# Optimizing a Trainium2 kernel written in Bass

```python
import numpy as np
import jax
import jax.numpy as jnp

def _softmax(x, axis=-1):
    return jax.nn.softmax(x, axis=axis)

def _gelu(x):
    return jax.nn.gelu(x, approximate=True)

def _silu(x):
    return jax.nn.silu(x)

def _sigmoid(x):
    return jax.nn.sigmoid(x)

def _layernorm(x, axis=-1, eps=1e-05):
    m = jnp.mean(x, axis=axis, keepdims=True)
    v = jnp.var(x, axis=axis, keepdims=True)
    return (x - m) / jnp.sqrt(v + eps)

def _scatter_add(tgt, idx, src, axis=0):
    return tgt.at[idx].add(src)

def _segment_sum(src, seg, n):
    return jax.ops.segment_sum(src, seg, n)
kernel_name = 'mk_cond_resid_d2_seqx_r8_5bebac'

def setup_inputs(seed: int=0):
    np.random.seed(seed)
    _w = jnp.asarray

    def _rec_inputs():
        import jax
        import jax.numpy as jnp
        _rk = jax.random.key(seed)
        x = 7.22e-05 + 1 * jax.random.normal(jax.random.fold_in(_rk, 1), (16, 128, 256), jnp.float32)
        _lenS = 128 - jax.random.randint(jax.random.fold_in(_rk, 7), (16,), 0, max(1, 128 // 4) + 1, jnp.int32)
        _lenS2 = 128 - jax.random.randint(jax.random.fold_in(_rk, 8), (16,), 0, max(1, 128 // 4) + 1, jnp.int32)
        cond_2048 = jax.random.bernoulli(jax.random.fold_in(_rk, 11), 0.5063, (16, 256)).astype(jnp.float32)
        return (x, cond_2048)
    x, cond_2048 = _rec_inputs()

    def _L0_cond_setup():
        import jax, jax.numpy as jnp
        import numpy as np
        NH = 8
        NEG = -1e+30
        key = jax.random.key(seed)
        k1, k2, k3, k4 = jax.random.split(key, 4)
        B, D, T = (4, 128, 256)
        x = jax.random.normal(k1, (B, D, T), dtype=jnp.float32)
        mask = jax.random.randint(k2, (B, T), 0, 2).astype(jnp.float32)
        lim = float(np.sqrt(6.0 / (D + D)))
        Wq = jax.random.uniform(k3, (D, D), dtype=jnp.float32, minval=-lim, maxval=lim)
        Wo = jax.random.uniform(k4, (D, D), dtype=jnp.float32, minval=-lim, maxval=lim)
        return {'x': x, 'mask': mask, 'Wq': Wq, 'Wo': Wo}
    _L0_cond_all = _L0_cond_setup()
    _L0_cond_in = {k: v for k, v in _L0_cond_all.items() if k in ('Wq', 'Wo')}
    del _L0_cond_all

    def _L1_cond_setup():
        import jax, jax.numpy as jnp
        import numpy as np
        DIM = 256
        H = 16
        DH = 128
        INNER = H * DH
        MLP = 4 * DIM
        B, T = (2, 256)
        EPS = 1e-06

        def _ln(x):
            mu = jnp.mean(x, axis=-1, keepdims=True)
            var = jnp.var(x, axis=-1, keepdims=True)
            return (x - mu) * jax.lax.rsqrt(var + EPS)
        key = jax.random.key(seed)
        ks = jax.random.split(key, 12)
        s = 0.02
        return {'x': jax.random.normal(ks[0], (B, T, DIM), jnp.float32), 'timestep_embed': jax.random.normal(ks[1], (B, DIM), jnp.float32), 'ada_w': jax.random.normal(ks[2], (DIM, 6 * DIM), jnp.float32) * s, 'ada_b': jnp.zeros((6 * DIM,), jnp.float32), 'qkv_w': jax.random.normal(ks[3], (DIM, 3 * INNER), jnp.float32) * s, 'qkv_b': jnp.zeros((3 * INNER,), jnp.float32), 'out_w': jax.random.normal(ks[4], (INNER, DIM), jnp.float32) * s, 'out_b': jnp.zeros((DIM,), jnp.float32), 'ffn_w1': jax.random.normal(ks[5], (DIM, MLP), jnp.float32) * s, 'ffn_b1': jnp.zeros((MLP,), jnp.float32), 'ffn_w2': jax.random.normal(ks[6], (MLP, DIM), jnp.float32) * s, 'ffn_b2': jnp.zeros((DIM,), jnp.float32)}
    _L1_cond_all = _L1_cond_setup()
    _L1_cond_in = {k: v for k, v in _L1_cond_all.items() if k in ('ada_w', 'ada_b', 'qkv_w', 'qkv_b', 'out_w', 'out_b', 'ffn_w1', 'ffn_b1', 'ffn_w2', 'ffn_b2')}
    del _L1_cond_all
    return {'x': x, 'cond_2048': cond_2048, 'L0_cond_Wq': _L0_cond_in['Wq'], 'L0_cond_Wo': _L0_cond_in['Wo'], 'L1_cond_ada_w': _L1_cond_in['ada_w'], 'L1_cond_ada_b': _L1_cond_in['ada_b'], 'L1_cond_qkv_w': _L1_cond_in['qkv_w'], 'L1_cond_qkv_b': _L1_cond_in['qkv_b'], 'L1_cond_out_w': _L1_cond_in['out_w'], 'L1_cond_out_b': _L1_cond_in['out_b'], 'L1_cond_ffn_w1': _L1_cond_in['ffn_w1'], 'L1_cond_ffn_b1': _L1_cond_in['ffn_b1'], 'L1_cond_ffn_w2': _L1_cond_in['ffn_w2'], 'L1_cond_ffn_b2': _L1_cond_in['ffn_b2']}

def reference(x, cond_2048, L0_cond_Wq, L0_cond_Wo, L1_cond_ada_w, L1_cond_ada_b, L1_cond_qkv_w, L1_cond_qkv_b, L1_cond_out_w, L1_cond_out_b, L1_cond_ffn_w1, L1_cond_ffn_b1, L1_cond_ffn_w2, L1_cond_ffn_b2):
    import jax
    import jax.numpy as jnp

    def _L0_cond_ref(x, mask, Wq, Wo):
        import jax, jax.numpy as jnp
        import numpy as np
        NH = 8
        NEG = -1e+30
        B, D, T = x.shape
        dk = D // NH
        scale = 1.0 / jnp.sqrt(jnp.asarray(dk, x.dtype))
        xt = jnp.transpose(x, (0, 2, 1))
        q = xt @ Wq.T
        qh = q.reshape(B, T, NH, dk).transpose(0, 2, 1, 3)
        scores = scale * jnp.einsum('bhqd,bhkd->bhqk', qh, qh)
        cmask = mask[:, None, None, :]
        rmask = mask[:, None, :, None]
        logits = (scores * cmask + (1.0 - cmask) * NEG) * rmask
        attn = jax.nn.softmax(logits, axis=-1)
        ctx = jnp.einsum('bhqk,bhkd->bhqd', attn, qh)
        ctx = ctx.transpose(0, 2, 1, 3).reshape(B, T, D)
        out = ctx @ Wo.T
        return jnp.transpose(out, (0, 2, 1))

    def _L1_cond_ref(x, timestep_embed, ada_w, ada_b, qkv_w, qkv_b, out_w, out_b, ffn_w1, ffn_b1, ffn_w2, ffn_b2):
        import jax, jax.numpy as jnp
        import numpy as np
        DIM = 256
        H = 16
        DH = 128
        INNER = H * DH
        MLP = 4 * DIM
        B, T = (2, 256)
        EPS = 1e-06

        def _ln(x):
            mu = jnp.mean(x, axis=-1, keepdims=True)
            var = jnp.var(x, axis=-1, keepdims=True)
            return (x - mu) * jax.lax.rsqrt(var + EPS)
        Bc, Tc, D = x.shape
        ada = (timestep_embed @ ada_w + ada_b)[:, None, :]
        shift1, scale1, gate1, shift2, scale2, gate2 = jnp.split(ada, 6, axis=-1)
        x1 = _ln(x) * (1.0 + scale1) + shift1
        qkv = (x1 @ qkv_w + qkv_b).reshape(Bc, Tc, 3, H, DH)
        q, k, v = (qkv[:, :, 0], qkv[:, :, 1], qkv[:, :, 2])
        scale = DH ** (-0.5)
        attn = jnp.einsum('bthd,bshd->bhts', q, k) * scale
        attn = jax.nn.softmax(attn, axis=-1)
        attn_out = jnp.einsum('bhts,bshd->bthd', attn, v).reshape(Bc, Tc, INNER)
        attn_out = attn_out @ out_w + out_b
        x = x + gate1 * attn_out
        x2 = _ln(x) * (1.0 + scale2) + shift2
        h = jax.nn.gelu(x2 @ ffn_w1 + ffn_b1, approximate=False)
        x = x + gate2 * (h @ ffn_w2 + ffn_b2)
        return x
    x = x + _L0_cond_ref(x, cond_2048, L0_cond_Wq, L0_cond_Wo)
    x = x + _L1_cond_ref(x, cond_2048, L1_cond_ada_w, L1_cond_ada_b, L1_cond_qkv_w, L1_cond_qkv_b, L1_cond_out_w, L1_cond_out_b, L1_cond_ffn_w1, L1_cond_ffn_b1, L1_cond_ffn_w2, L1_cond_ffn_b2)
    return x

_drawn_inputs = setup_inputs


def setup_inputs(seed=0):
    import zlib

    import numpy as np

    out = dict(_drawn_inputs(seed))
    spreads = {'L1_cond_ada_b': (0.0, 0.765),
     'L1_cond_qkv_b': (0.0, 0.709),
     'L1_cond_out_b': (0.0, 0.709),
     'L1_cond_ffn_b1': (0.0, 0.8),
     'L1_cond_ffn_b2': (0.0, 0.68)}
    factors = {'L1_cond_qkv_w': 6.023,
     'L1_cond_out_w': 3.813,
     'L1_cond_ffn_w1': 4.302,
     'L1_cond_ffn_w2': 3.969}
    for name, (base, spread) in spreads.items():
        noise = np.random.default_rng([zlib.crc32(name.encode()), seed]).standard_normal(out[name].shape)
        drawn = base * np.exp(spread * noise) if base else spread * noise
        out[name] = jnp.asarray(drawn.astype(out[name].dtype))
    for name, factor in factors.items():
        out[name] = (out[name] * factor).astype(out[name].dtype)
    return out
```

```python
from contextlib import ExitStack

import concourse.bass as bass
from concourse import mybir

ALU = mybir.AluOpType
ACT = mybir.ActivationFunctionType
F32 = mybir.dt.float32
F32R = mybir.dt.float32r
I32 = mybir.dt.int32
AX_X = mybir.AxisListType.X

P = 128
B, T, DIM = 16, 128, 256
NH, DK = 8, 16
UNITS = B // 2 * 4
NEG = -1e30
H, DH = 16, 128
KT = DIM // P
INNER = H * DH
MLP = 4 * DIM
MC = MLP // P
GB = 4
NG = B // GB
GT = GB * T
ROWS_ONE = 48
EPS = 1e-6
QKV_COLS = KT * 3 * INNER
W_COLS = QKV_COLS + H * DIM
CHUNK = 1024
SC = DH ** -0.5
FFN_COLS = KT * MLP + MC * DIM
X2_COL = FFN_COLS
HID_COL = X2_COL + KT * B * T
C_AQ, C_AK, C_BH, C_RA, C_CA, C_CB, C_ID = 0, 1, 2, 3, 4, 5, 8


def wait(eng, sem, value):
    if not isinstance(value, int) or value > 0:
        eng.wait_ge(sem, value)


def build(nc, x, cond, Wq, Wo, ada_w, ada_b, qkv_w, qkv_b, out_w, out_b, ffn_w1, ffn_b1, ffn_w2, ffn_b2, consts, out):
    top = ExitStack()

    def sem(name):
        return top.enter_context(nc.semaphore(name))

    def sb(ctx, name, shape, dt=F32):
        return ctx.enter_context(nc.sbuf_tensor(name, shape, dt))

    with top:
        X = sb(top, "X", [P, B, DIM])
        w_hi = sb(top, "w_hi", [P, W_COLS], F32R)
        w_lo = sb(top, "w_lo", [P, W_COLS], F32R)
        cst = sb(top, "cst", [P, C_ID + P])
        ada = sb(top, "ada", [P, 12, B])
        gb1 = sb(top, "gb1", [P, KT, B])
        gb2 = sb(top, "gb2", [P, KT, B])
        qkvb = sb(top, "qkvb", [P, 3, H])
        qb_s = sb(top, "qb_s", [P, H])
        adab = sb(top, "adab", [P, 12])
        ob = sb(top, "ob", [P, KT])
        b1 = sb(top, "b1", [P, MC])
        b2 = sb(top, "b2", [P, KT])
        ident = cst[:, C_ID:C_ID + P]
        psum = [top.enter_context(nc.psum_tensor(f"bank{i}", [P, 512], F32)) for i in range(4)]
        ring = top.enter_context(nc.psum_tensor("ring", [P, 4, 512], F32))
        banks = psum + [ring[:, i, :] for i in range(4)]

        first_block(nc, sem, sb, x, cond, Wq, Wo, ada_w, ada_b, qkv_w, qkv_b, out_w, out_b, ffn_b1, ffn_b2,
                    consts, X, w_hi, w_lo, cst, ada, gb1, gb2, qkvb, qb_s, adab, ob, b1, b2, ident, psum, ring)
        kept = nc.dram_tensor("kept", (B, T, DIM), F32).ap()
        saved = sem("saved")
        with ExitStack() as ctx:
            x1f = sb(ctx, "x1f", [P, KT, B * T])
            layernorm(nc, sem, sb, "one", X, ada, 2, 0, ident, banks, x1f, save=(kept, saved))
            attention(nc, sem, sb, saved, x1f, X, w_hi, w_lo, ada, gb1, qkvb, qb_s, ident, banks)
        with ExitStack() as ctx:
            x2f = sb(ctx, "x2f", [P, KT, B * T])
            raw = sb(ctx, "raw", [P, FFN_COLS])
            layernorm(nc, sem, sb, "two", X, ada, 8, 6, ident, banks, x2f,
                      ffn_weights=(ffn_w1, ffn_w2, raw, w_hi, w_lo))
            ffn(nc, sem, sb, kept, x2f, X, w_hi, w_lo, ada, gb2, b1, ident, banks, out)


def first_block(nc, sem, sb, x, cond, Wq, Wo, ada_w, ada_b, qkv_w, qkv_b, out_w, out_b, ffn_b1, ffn_b2,
                consts, X, w_hi, w_lo, cst, ada, gb1, gb2, qkvb, qb_s, adab, ob, b1, b2, ident, psum, ring):
    vbank, tbank, O = psum[0], psum[1], [psum[2], psum[3]]
    with ExitStack() as ctx:
        wqo = sb(ctx, "wqo", [P, 2, P])
        wqoT = sb(ctx, "wqoT", [P, 2, P])
        wst = sb(ctx, "wst", [P, 4, P])
        cnd = sb(ctx, "cnd", [B, DIM])
        cndT = sb(ctx, "cndT", [P, KT, B])
        mb = sb(ctx, "mb", [P, 512])
        R = sb(ctx, "R", [P, 512])
        C = sb(ctx, "C", [P, 512])
        xs = sb(ctx, "xs", [P, 512])
        hs = sb(ctx, "hs", [P, 512], F32R)
        qst = sb(ctx, "qst", [P, 4, 512], F32R)
        kst = sb(ctx, "kst", [P, 4, 512], F32R)
        qst2 = sb(ctx, "qst2", [P, 512], F32R)
        mcol = sb(ctx, "mcol", [P, 4, P])
        pt = sb(ctx, "pt", [P, 2, 1024])
        V = sb(ctx, "V", [P, 4, NH, DK + 1])
        rin = sb(ctx, "rin", [P, 2, 2 * NH])
        ctxs = sb(ctx, "ctxs", [P, 4, P])
        ctxT = sb(ctx, "ctxT", [P, 512])
        stage = sb(ctx, "stage", [P, 2, CHUNK])

        l_small, l_w, l_x0, l_x, l_ada, l_mb, l_xs = (sem(n) for n in (
            "l_small", "l_w", "l_x0", "l_x", "l_ada", "l_mb", "l_xs"))
        l_st = [sem("l_st0"), sem("l_st1")]
        pe_wT, wT_done, pe_ada, ada_done, set_done, wst_done, pool_set = (sem(n) for n in (
            "pe_wT", "wT_done", "pe_ada", "ada_done", "set_done", "wst_done", "pool_set"))
        pe_proj, act_h, dve_st, pool_st, pe_s, dve_max, pe_t, dve_q2, pe_st, act_exp, pe_pv = (sem(n) for n in (
            "pe_proj", "act_h", "dve_st", "pool_st", "pe_s", "dve_max", "pe_t", "dve_q2", "pe_st", "act_exp", "pe_pv"))
        pe_v, act_v, dve_rin, dve_ctx, pe_ctxT, act_ctxT, pe_out, dve_x, dve_rc, act_hi, pool_lo = (sem(n) for n in (
            "pe_v", "act_v", "dve_rin", "dve_ctx", "pe_ctxT", "act_ctxT", "pe_out", "dve_x", "dve_rc", "act_hi",
            "pool_lo"))

        qkv_v = qkv_w.rearrange("(k p) n -> p k n", p=P)
        outw_v = out_w.rearrange("(h p) n -> p h n", p=P)
        NGR = UNITS // 4

        def run(eng, step):
            for n in range(-3, 4):
                step(n // 4, n % 4)
            with eng.Fori(1, NGR - 1) as g:
                for t in range(4):
                    step(g, t)
            for n in range(UNITS - 4, UNITS + 2):
                step(n // 4, n % 4)

        def unit(g, t, ahead):
            u = g * 4 + t + ahead
            if isinstance(u, int) and not 0 <= u < UNITS:
                return None, None
            return u, (t + ahead) % 4

        def pair(g):
            return not isinstance(g, int) or 0 <= g < NGR

        with nc.Block() as block:

            @block.sync
            def _(sp):
                sp.dma_start(cst[:, :], consts).then_inc(l_small, 16)
                sp.dma_start(wqo[:, 0, :], Wq).then_inc(l_w, 16)
                sp.dma_start(wqo[:, 1, :], Wo).then_inc(l_w, 16)
                sp.dma_start(cnd[:, :], cond).then_inc(l_w, 16)
                sp.dma_start(X[:, 0:2, :], x[0:2].rearrange("b p d -> p b d")).then_inc(l_x0, 16)

                def mask(g):
                    wait(sp, dve_rc, g)
                    src = cond[2 * g:2 * g + 2, :].rearrange("b d -> (b d)").partition_broadcast(P)
                    sp.dma_start(mb[:, :], src).then_inc(l_mb, 16)

                def statics(g):
                    wait(sp, pe_v, g)
                    sp.dma_start(xs[:, :].rearrange("p (b d) -> p b d", b=2),
                                 x[2 * g:2 * g + 2].rearrange("b p d -> p b d")).then_inc(l_xs, 16)

                mask(0)
                statics(0)
                sp.dma_start(pt[:, :, :].rearrange("p a n -> p (a n)")[:, 0:6 * DIM], ada_w[0:P, :]).then_inc(l_ada, 16)
                sp.dma_start(stage[:, :, :].rearrange("p a n -> p (a n)")[:, 0:6 * DIM],
                             ada_w[P:2 * P, :]).then_inc(l_ada, 16)
                sp.dma_start(X[:, 2:B, :], x[2:B].rearrange("b p d -> p b d")).then_inc(l_x, 16)
                for dst, src, n in ((adab, ada_b, 12), (ob, out_b, KT), (b1, ffn_b1, MC), (b2, ffn_b2, KT)):
                    sp.dma_start(dst[:, :], src.rearrange("(n p) -> p n", p=P),
                                 allow_slow_non_contiguous=True).then_inc(l_small, 16)
                sp.dma_start(qkvb[:, :, :], qkv_b.rearrange("(s h p) -> p s h", s=3, p=P),
                             allow_slow_non_contiguous=True).then_inc(l_small, 16)
                for c in range(W_COLS // CHUNK):
                    if c < 2:
                        sp.wait_ge(ada_done, 1)
                    else:
                        sp.wait_ge(pool_lo, 2 * (c - 1))
                    if c < QKV_COLS // CHUNK:
                        k, n = divmod(c, 3 * INNER // CHUNK)
                        src = qkv_v[:, k, n * CHUNK:(n + 1) * CHUNK]
                        dst = stage[:, c % 2, :]
                    else:
                        n = c - QKV_COLS // CHUNK
                        src = outw_v[:, n * 4:n * 4 + 4, :]
                        dst = stage[:, c % 2, :].rearrange("p (h n) -> p h n", h=4)
                    sp.dma_start(dst, src).then_inc(l_st[c % 2], 16)
                    if c % 2 == 1 and c // 2 + 1 < NGR:
                        mask(c // 2 + 1)
                        statics(c // 2 + 1)

            @block.gpsimd
            def _(pool):
                pool.memset(mcol[:, :, :], 0.0)
                pool.memset(wst[:, :, :], 0.0)
                pool.memset(V[:, :, :, :], 1.0).then_inc(pool_set, 1)

                def step(g, t):
                    u, j = unit(g, t, 3)
                    if u is not None:
                        if t == 1:
                            wait(pool, dve_rc, g + 2)
                        wait(pool, dve_st, u + 1)
                        pool.tensor_tensor(qst[:, j, :], qst[:, j, :].bitcast(F32), R[:, :], ALU.mult)
                        pool.tensor_tensor(kst[:, j, :], kst[:, j, :].bitcast(F32), C[:, :],
                                           ALU.mult).then_inc(pool_st, 1)
                    n, _ = unit(g, t, 0)
                    if n is not None:
                        wait(pool, act_hi, n + 1)
                        cols = bass.ds(n * 512, 512)
                        pool.tensor_tensor(w_lo[:, cols], stage[:, t // 2, t % 2 * 512:t % 2 * 512 + 512],
                                           w_hi[:, cols].bitcast(F32), ALU.subtract).then_inc(pool_lo, 1)

                run(pool, step)

            @block.tensor
            def _(pe):
                pe.wait_ge(l_small, 96)
                pe.wait_ge(l_w, 48)
                for i in range(2):
                    nc.tensor.transpose(tbank[:, i * P:(i + 1) * P], wqo[:, i, :], ident)
                for k in range(KT):
                    last = nc.tensor.transpose(tbank[:, 256 + k * B:256 + (k + 1) * B], cnd[:, k * P:(k + 1) * P],
                                               ident[0:B, 0:B])
                last.then_inc(pe_wT, 1)
                pe.wait_ge(wT_done, 1)
                pe.wait_ge(l_ada, 32)
                aw = [pt[:, :, :].rearrange("p a n -> p (a n)"), stage[:, :, :].rearrange("p a n -> p (a n)")]
                for m in range(12):
                    for k in range(KT):
                        last = nc.tensor.matmul(vbank[:, m * B:(m + 1) * B], aw[k][:, m * P:(m + 1) * P],
                                                cndT[:, k, :], start=(k == 0), stop=(k == KT - 1))
                last.then_inc(pe_ada, 1)
                pe.wait_ge(ada_done, 1)
                pe.wait_ge(wst_done, 1)
                pe.wait_ge(pool_set, 1)
                pe.wait_ge(l_x0, 16)

                def values(g):
                    wait(pe, l_xs, 16 * (g + 1))
                    for bk in range(4):
                        last = nc.tensor.matmul(tbank[:, bk * P:(bk + 1) * P], xs[:, bk * P:(bk + 1) * P],
                                                wqoT[:, 0, :], start=True, stop=True)
                    last.then_inc(pe_v, 1)

                def pv(n, j, b):
                    for s in range(2):
                        for qt in range(2):
                            col = qt * 8 * (DK + 1) + (2 * j + s) * (DK + 1)
                            for kt in range(2):
                                p0 = (s * 2 + kt) * 256 + qt * P
                                last = nc.tensor.matmul(O[b][:, col:col + DK + 1], pt[:, b, p0:p0 + P],
                                                        V[:, b * 2 + kt, 2 * j + s, :], start=(kt == 0),
                                                        stop=(kt == 1))
                    last.then_inc(pe_pv, 1)

                def step(g, t):
                    n, j = unit(g, t, 0)
                    if n is not None:
                        if t == 0:
                            wait(pe, act_v, g + 1)
                            wait(pe, dve_ctx, g)
                        wait(pe, act_exp, 2 * n + 1)
                        pv(n, j, 0)
                    u, _ = unit(g, t, 1)
                    if u is not None:
                        wait(pe, dve_max, 2 * u + 2)
                        if t == 0:
                            wait(pe, act_v, g + 1)
                        elif t == 1 and pair(g - 1):
                            wait(pe, act_ctxT, g)
                        elif t == 2 and pair(g - 1):
                            wait(pe, dve_x, g)
                        for i in range(4):
                            last = nc.tensor.transpose(tbank[:, i * P:(i + 1) * P], mcol[:, i, :], ident)
                        last.then_inc(pe_t, 1)
                    if n is not None:
                        wait(pe, act_exp, 2 * n + 2)
                        pv(n, j, 1)
                    if u is not None:
                        wait(pe, dve_q2, u + 1)
                    if t == 0 and pair(g - 1):
                        wait(pe, dve_ctx, g)
                        for i in range(4):
                            last = nc.tensor.transpose(tbank[:, i * P:(i + 1) * P], ctxs[:, i, :], ident)
                        last.then_inc(pe_ctxT, 1)
                    if t == 1 and pair(g - 1):
                        wait(pe, act_ctxT, g)
                        nc.tensor.matmul(tbank[:, :], wqoT[:, 1, :], ctxT[:, :], start=True,
                                         stop=True).then_inc(pe_out, 1)
                    if t == 3 and pair(g + 1):
                        values(g + 1)
                    if u is not None:
                        ju = (t + 1) % 4
                        for b in range(2):
                            for kt in range(2):
                                for s in range(2):
                                    r = slice(64 * s, 64 * s + 64)
                                    k0 = b * 256 + kt * P
                                    last = nc.tensor.matmul(ring[:, 2 * b + s, kt * 256:kt * 256 + 256],
                                                            kst[r, ju, k0:k0 + P], qst2[r, b * 256:b * 256 + 256],
                                                            start=True, stop=True)
                            last.then_inc(pe_st, 1)
                    u, ju = unit(g, t, 3)
                    if u is not None:
                        wait(pe, dve_st, u)
                        if t == 1 and isinstance(g, int) and g == 0:
                            pe.wait_ge(l_x, 16)
                        gx = g if t == 0 else g + 1
                        nc.tensor.matmul(vbank[:, :].rearrange("p (b d) -> p b d", b=2), wst[:, ju, :],
                                         X[:, bass.ds(gx * 2, 2), :], start=True, stop=True).then_inc(pe_proj, 1)
                    u, ju = unit(g, t, 2)
                    if u is not None:
                        wait(pe, pool_st, u + 1)
                        for b in range(2):
                            wait(pe, act_exp, 2 * (u - 1) + b + 1)
                            for qt in range(2):
                                for s in range(2):
                                    r = slice(64 * s, 64 * s + 64)
                                    q0 = b * 256 + qt * P
                                    last = nc.tensor.matmul(ring[:, 2 * b + s, qt * 256:qt * 256 + 256],
                                                            qst[r, ju, q0:q0 + P], kst[r, ju, b * 256:b * 256 + 256],
                                                            start=True, stop=True)
                            last.then_inc(pe_s, 1)

                run(pe, step)

            @block.scalar
            def _(act):
                def step(g, t):
                    if t == 0 and pair(g - 1):
                        wait(act, pe_ctxT, g)
                        nc.scalar.copy(ctxT[:, :], tbank[:, :]).then_inc(act_ctxT, 1)
                    if t == 3 and pair(g + 1):
                        wait(act, pe_v, g + 2)
                        if isinstance(g, int) and g == -1:
                            act.wait_ge(pool_set, 1)
                        nc.scalar.copy(V[:, :, :, 0:DK],
                                       tbank[:, :].rearrange("p (k h d) -> p k h d", k=4, h=NH)).then_inc(act_v, 1)
                    u, _ = unit(g, t, 1)
                    if u is not None:
                        for b in range(2):
                            wait(act, pe_st, 2 * u + b + 1)
                            wait(act, pe_pv, 2 * (u - 1) + b + 1)
                            nc.scalar.activation(pt[:, b, :], ring[:, 2 * b:2 * b + 2, :], ACT.Exp,
                                                 scale=DK ** -0.5).then_inc(act_exp, 1)
                    u, _ = unit(g, t, 3)
                    if u is not None:
                        wait(act, pe_proj, u + 1)
                        nc.scalar.activation(hs[:, :], vbank[:, :], ACT.Identity,
                                             bias=cst[:, C_BH:C_BH + 1]).then_inc(act_h, 1)
                    n, _ = unit(g, t, 0)
                    if n is not None:
                        wait(act, l_st[t // 2], 16 * (g + 1))
                        nc.scalar.copy(w_hi[:, bass.ds(n * 512, 512)],
                                       stage[:, t // 2, t % 2 * 512:t % 2 * 512 + 512]).then_inc(act_hi, 1)

                run(act, step)

            @block.vector
            def _(dve):
                count = [0]

                def chain(ins):
                    count[0] += 1
                    ins.then_inc(set_done, 1)
                    dve.wait_ge(set_done, count[0])

                dve.wait_ge(pe_wT, 1)
                chain(dve.tensor_copy(wqoT[:, :, :], tbank[:, 0:256].rearrange("p (i n) -> p i n", i=2)))
                dve.tensor_copy(cndT[:, :, :], tbank[:, 256:256 + KT * B].rearrange("p (k n) -> p k n", k=KT)
                                ).then_inc(wT_done, 1)
                dve.wait_ge(pool_set, 1)
                wv = wst[:, :, :].rearrange("p j (s e d) -> p (j s) e d", s=2, d=DK)
                for slot in range(3):
                    last = dve.tensor_copy(wv[:, :, slot, :], wqoT[:, 0, :].rearrange("p (h d) -> p h d", h=NH))
                last.then_inc(wst_done, 1)
                dve.wait_ge(pe_ada, 1)
                chain(dve.tensor_tensor(ada[:, :, :], vbank[:, 0:12 * B].rearrange("p (m b) -> p m b", m=12),
                                        adab[:, :, None].to_broadcast([P, 12, B]), ALU.add))
                chain(dve.tensor_scalar(ada[:, 2:4, :], ada[:, 2:4, :], 1.0, None, ALU.add))
                chain(dve.tensor_scalar(ada[:, 8:10, :], ada[:, 8:10, :], 1.0, None, ALU.add))
                chain(dve.tensor_tensor(gb1[:, :, :], ada[:, 4:6, :], ob[:, :, None].to_broadcast([P, KT, B]), ALU.mult))
                chain(dve.tensor_tensor(gb2[:, :, :], ada[:, 10:12, :], b2[:, :, None].to_broadcast([P, KT, B]),
                                        ALU.mult))
                dve.tensor_scalar(qb_s[:, :], qkvb[:, 0, :], SC, None, ALU.mult).then_inc(ada_done, 1)

                def step(g, t):
                    if t == 0 and pair(g - 1):
                        wait(dve, pe_pv, 8 * g)
                        ov = [o[:, 0:16 * (DK + 1)].rearrange("p (h d) -> p h d", d=DK + 1) for o in O]
                        for b in range(2):
                            last = dve.reciprocal(rin[:, b, :], ov[b][:, :, DK])
                        last.then_inc(dve_rin, 1)
                        wait(dve, dve_rin, g)
                        for b in range(2):
                            last = dve.tensor_tensor(
                                ctxs[:, 2 * b:2 * b + 2, :].rearrange("p q (h d) -> p (q h) d", d=DK),
                                ov[b][:, :, 0:DK], rin[:, b, :, None].to_broadcast([P, 2 * NH, DK]), ALU.mult)
                        last.then_inc(dve_ctx, 1)
                    u, ju = unit(g, t, 1)
                    if u is not None:
                        wait(dve, pe_t, u + 1)
                        dve.tensor_tensor(qst2[:, :], tbank[:, :], qst[:, ju, :].bitcast(F32),
                                          ALU.add).then_inc(dve_q2, 1)
                    if t == 1 and pair(g - 1):
                        wait(dve, pe_out, g)
                        xg = X[:, bass.ds(g * 2 - 2, 2), :]
                        dve.tensor_tensor(xg, tbank[:, :].rearrange("p (b d) -> p b d", b=2), xg,
                                          ALU.add).then_inc(dve_x, 1)
                    if t == 1 and pair(g + 1):
                        wait(dve, pool_st, 4 * g + 4)
                        wait(dve, l_mb, 16 * (g + 2))
                        dve.tensor_scalar(R[:, :], mb[:, :], cst[:, C_RA:C_RA + 1], None, ALU.mult)
                        dve.tensor_scalar(C[:, :], mb[:, :], cst[:, C_CA:C_CA + 1], cst[:, C_CB:C_CB + 1],
                                          ALU.mult, ALU.add).then_inc(dve_rc, 1)
                    u, ju = unit(g, t, 3)
                    if u is not None:
                        wait(dve, act_h, u + 1)
                        h = hs[:, :].bitcast(F32)
                        dve.scalar_tensor_tensor(qst[:, ju, :], h, cst[:, C_AQ:C_AQ + 1], vbank[:, :],
                                                 ALU.mult, ALU.add)
                        dve.scalar_tensor_tensor(kst[:, ju, :], h, cst[:, C_AK:C_AK + 1], vbank[:, :],
                                                 ALU.mult, ALU.add).then_inc(dve_st, 1)
                    u, _ = unit(g, t, 2)
                    if u is not None:
                        for b in range(2):
                            wait(dve, pe_s, 2 * u + b + 1)
                            dst = mcol[:, 2 * b:2 * b + 2, :].rearrange("p q (s r) -> p s q r", s=2)[
                                :, :, :, ROWS_ONE + 1]
                            src = ring[:, 2 * b:2 * b + 2, :].rearrange("p s (q k) -> p s q k", q=2)
                            dve.tensor_reduce(dst, src, AX_X, ALU.max, negate=True).then_inc(dve_max, 1)

                run(dve, step)



def layernorm(nc, sem, sb, tag, X, ada, scale0, shift0, ident, banks, xf, ffn_weights=None, save=None):
    with ExitStack() as ctx:
        xn = sb(ctx, f"xn_{tag}", [P, B, DIM])
        bst = sb(ctx, f"bst_{tag}", [P, B, 6])
        mv = sb(ctx, f"mv_{tag}", [P, B, 2])
        ve = sb(ctx, f"ve_{tag}", [P, B])
        rst = sb(ctx, f"rst_{tag}", [P, B])
        nwt = sb(ctx, f"nwt_{tag}", [P, B])
        chained, dve_xn, pe_xt, act_m, dve_m, l_raw, act_whi, pool_wlo = (sem(f"{n}_{tag}") for n in (
            "chained", "dve_xn", "pe_xt", "act_m", "dve_m", "l_raw", "act_whi", "pool_wlo"))
        with nc.Block() as block:

            if save:
                @block.sync
                def _(sp):
                    sp.dma_start(save[0].rearrange("b p d -> p b d"), X[:, :, :]).then_inc(save[1], 16)

            if ffn_weights:
                w1, w2, raw, w_hi, w_lo = ffn_weights

                @block.sync
                def _(sp):
                    sp.dma_start(raw[:, 0:KT * MLP].rearrange("p (k n) -> p k n", k=KT),
                                 w1.rearrange("(k p) n -> p k n", p=P)).then_inc(l_raw, 16)
                    sp.dma_start(raw[:, KT * MLP:FFN_COLS].rearrange("p (c n) -> p c n", c=MC),
                                 w2.rearrange("(c p) n -> p c n", p=P)).then_inc(l_raw, 16)

                @block.gpsimd
                def _(pool):
                    for i in range(2):
                        cols = slice(i * KT * MLP, (i + 1) * KT * MLP)
                        pool.wait_ge(act_whi, i + 1)
                        pool.tensor_tensor(w_lo[:, cols], raw[:, cols], w_hi[:, cols].bitcast(F32),
                                           ALU.subtract).then_inc(pool_wlo, 1)

            @block.tensor
            def _(pe):
                for g in range(NG):
                    for b in range(GB):
                        pe.wait_ge(dve_xn, g * GB + b + 1)
                        for k in range(KT):
                            last = nc.tensor.transpose(banks[2 * g + k][:, b * T:(b + 1) * T],
                                                       xn[:, g * GB + b, k * P:(k + 1) * P], ident)
                    last.then_inc(pe_xt, 1)

            @block.scalar
            def _(act):
                if ffn_weights:
                    act.wait_ge(l_raw, 32)
                    for i in range(2):
                        cols = slice(i * KT * MLP, (i + 1) * KT * MLP)
                        nc.scalar.copy(w_hi[:, cols], raw[:, cols]).then_inc(act_whi, 1)
                for g in range(NG):
                    act.wait_ge(pe_xt, g + 1)
                    for b in range(GB * g, GB * g + GB):
                        last = nc.scalar.activation(xf[:, 0, b * T:(b + 1) * T],
                                                    banks[2 * g][:, (b - GB * g) * T:(b - GB * g + 1) * T],
                                                    ACT.Identity, bias=ada[:, shift0, b:b + 1],
                                                    scale=ada[:, scale0, b:b + 1])
                    last.then_inc(act_m, 1)

            @block.vector
            def _(dve):
                count = [0]

                def chain(ins):
                    count[0] += 1
                    ins.then_inc(chained, 1)
                    dve.wait_ge(chained, count[0])

                for b in range(B):
                    last = dve.bn_stats(bst[:, b, :], X[:, b, :])
                chain(last)
                for b in range(B):
                    last = dve.bn_aggr(mv[:, b, :], bst[:, b, :])
                chain(last)
                chain(dve.tensor_scalar(ve[:, :], mv[:, :, 1], EPS, None, ALU.add))
                chain(dve.tensor_scalar(rst[:, :].bitcast(I32), ve[:, :].bitcast(I32), -0.5, 1597463007.0,
                                        ALU.mult, ALU.add))
                for _ in range(4):
                    chain(dve.tensor_tensor(nwt[:, :], rst[:, :], rst[:, :], ALU.mult))
                    chain(dve.tensor_tensor(nwt[:, :], nwt[:, :], ve[:, :], ALU.mult))
                    chain(dve.tensor_scalar(nwt[:, :], nwt[:, :], -0.5, 1.5, ALU.mult, ALU.add))
                    chain(dve.tensor_tensor(rst[:, :], rst[:, :], nwt[:, :], ALU.mult))

                def modulate(g):
                    dve.wait_ge(pe_xt, g + 1)
                    for b in range(GB * g, GB * g + GB):
                        last = dve.tensor_scalar(xf[:, 1, b * T:(b + 1) * T],
                                                 banks[2 * g + 1][:, (b - GB * g) * T:(b - GB * g + 1) * T],
                                                 ada[:, scale0 + 1, b:b + 1], ada[:, shift0 + 1, b:b + 1],
                                                 ALU.mult, ALU.add)
                    last.then_inc(dve_m, 1)

                for g in range(NG):
                    for b in range(GB * g, GB * g + GB):
                        dve.tensor_scalar(xn[:, b, :], X[:, b, :], mv[:, b, 0:1], rst[:, b:b + 1],
                                          ALU.subtract, ALU.mult).then_inc(dve_xn, 1)
                    if g:
                        modulate(g - 1)
                modulate(NG - 1)


def products(nc, bank, w_hi, w_lo, x_hi, x_lo, start, stop, ks):
    terms = [(w, x, k) for k in ks for w, x in ((w_hi, x_hi), (w_hi, x_lo), (w_lo, x_hi))]
    for i, (w, x, k) in enumerate(terms):
        last = nc.tensor.matmul(bank, w(k), x(k), start=(start and i == 0), stop=(stop and i == len(terms) - 1))
    return last


def attention(nc, sem, sb, saved, x1f, X, w_hi, w_lo, ada, gb1, qkvb, qb_s, ident, banks):
    UN = NG * H
    Qb, Kb, Vb, Sb, Tb, Ob = banks[0:6]
    Yb = banks[6:8]
    with ExitStack() as ctx:
        x1h = sb(ctx, "x1h", [P, KT, GT], F32R)
        x1l = sb(ctx, "x1l", [P, KT, GT], F32R)
        Q = sb(ctx, "Q", [P, 2, GT])
        K = sb(ctx, "K", [P, 2, GT])
        V = sb(ctx, "Vv", [P, 2, GB, 2 * DH])
        probs = sb(ctx, "probs", [P, 2, GB, T])
        pT = sb(ctx, "pT", [P, GT])
        oh = sb(ctx, "oh", [P, GT], F32R)
        ol = sb(ctx, "ol", [P, GT], F32R)
        yg = sb(ctx, "yg", [P, KT, GT])
        nm = sb(ctx, "nm", [P, 2, GB])
        sums = sb(ctx, "sums", [P, 2, GB])
        rinv = sb(ctx, "rinv", [P, 2, GB])
        (act_x1, dve_x1, pe_q, act_q, pe_k, act_k, pe_vv, dve_v, pe_sc, dve_mx, act_ex, dve_ri, pool_p, pe_pt, dve_pt,
         pe_o, act_oh, dve_ol, pe_y, act_y, dve_y, pe_yt, dve_xa) = (sem(n) for n in (
             "act_x1", "dve_x1", "pe_q", "act_q", "pe_k", "act_k", "pe_vv", "dve_v", "pe_sc", "dve_mx", "act_ex",
             "dve_ri", "pool_p", "pe_pt", "dve_pt", "pe_o", "act_oh", "dve_ol", "pe_y", "act_y", "dve_y", "pe_yt",
             "dve_xa"))

        def run(eng, step):
            step(-1, H - 1)
            for h in range(H):
                step(0, h)
            with eng.Fori(1, NG - 1) as g:
                for h in range(H):
                    step(g, h)
            for h in range(H):
                step(NG - 1, h)
            for h in range(4):
                step(NG, h)

        def unit(g, h, ahead):
            u = g * H + h + ahead
            if isinstance(u, int) and not 0 <= u < UN:
                return None
            return u

        def group(g):
            return not isinstance(g, int) or 0 <= g < NG

        with nc.Block() as block:

            @block.tensor
            def _(pe):
                def project(bank, part, hd):
                    def w(t):
                        return lambda k: t[:, k * 3 * INNER + part * INNER + hd * DH:
                                           k * 3 * INNER + part * INNER + (hd + 1) * DH]
                    return products(nc, bank[:, :], w(w_hi), w(w_lo), lambda k: x1h[:, k, :], lambda k: x1l[:, k, :],
                                    True, True, range(KT))

                def step(g, h):
                    n, prev, nxt = unit(g, h, 0), unit(g, h, -1), unit(g, h, 1)
                    hn = (h + 1) % H
                    if prev is not None:
                        wait(pe, pool_p, prev + 1)
                        wait(pe, dve_pt, prev)
                        if h in (3, 4) and group(g - 1):
                            wait(pe, dve_xa, 2 * g + h - 4)
                        for b in range(GB):
                            last = nc.tensor.transpose(Tb[:, b * T:(b + 1) * T], probs[:, (h + 1) % 2, b, :], ident)
                        last.then_inc(pe_pt, 1)
                    if n is not None:
                        wait(pe, act_q, n + 1)
                        wait(pe, act_k, n + 1)
                        wait(pe, act_ex, n)
                        for b in range(GB):
                            t = slice(b * T, (b + 1) * T)
                            last = nc.tensor.matmul(Sb[:, t], Q[:, h % 2, t], K[:, h % 2, t], start=True, stop=True)
                        last.then_inc(pe_sc, 1)
                    if nxt is not None:
                        if hn == 0:
                            wait(pe, dve_x1, g + 2)
                        project(Qb, 0, hn).then_inc(pe_q, 1)
                    if prev is not None:
                        wait(pe, dve_pt, prev + 1)
                        wait(pe, dve_v, prev + (2 if h % 2 else 1))
                        wait(pe, dve_ol, prev)
                        for b in range(GB):
                            last = nc.tensor.matmul(Ob[:, b * T:(b + 1) * T],
                                                    V[:, (h - 1) % H // 2 % 2, b, (h + 1) % 2 * DH:
                                                      ((h + 1) % 2 + 1) * DH],
                                                    pT[:, b * T:(b + 1) * T], start=True, stop=True)
                        last.then_inc(pe_o, 1)
                    if h in (2, 3) and group(g - 1):
                        wait(pe, act_y, g)
                        wait(pe, dve_y, g)
                        if h == 3:
                            wait(pe, dve_xa, 2 * g - 1)
                        for b in range(2):
                            for d in range(KT):
                                t0 = (2 * (h - 2) + b) * T
                                last = nc.tensor.transpose(Tb[:, b * DIM + d * P:b * DIM + (d + 1) * P],
                                                           yg[:, d, t0:t0 + T], ident)
                        last.then_inc(pe_yt, 1)
                    if nxt is not None:
                        project(Kb, 1, hn).then_inc(pe_k, 1)
                        wait(pe, dve_v, nxt)
                        for i in range(2):
                            b = 2 * (hn % 2) + i
                            c0 = 2 * INNER + hn // 2 * 2 * DH
                            last = products(nc, Vb[:, i * 2 * DH:(i + 1) * 2 * DH],
                                            lambda k: x1h[:, k, b * T:(b + 1) * T],
                                            lambda k: x1l[:, k, b * T:(b + 1) * T],
                                            lambda k: w_hi[:, k * 3 * INNER + c0:k * 3 * INNER + c0 + 2 * DH],
                                            lambda k: w_lo[:, k * 3 * INNER + c0:k * 3 * INNER + c0 + 2 * DH],
                                            True, True, range(KT))
                        last.then_inc(pe_vv, 1)
                    if prev is not None:
                        hp = (h - 1) % H
                        wait(pe, dve_ol, prev + 1)
                        if hp == 0:
                            wait(pe, act_y, g)
                            wait(pe, dve_y, g)
                        for d in range(KT):
                            c = QKV_COLS + hp * DIM + d * P
                            last = products(nc, Yb[d][:, :], lambda k: w_hi[:, c:c + P], lambda k: w_lo[:, c:c + P],
                                            lambda k: oh[:, :], lambda k: ol[:, :], hp == 0, hp == H - 1, range(1))
                        last.then_inc(pe_y, 1)

                run(pe, step)

            @block.scalar
            def _(act):
                def step(g, h):
                    n, prev, nxt = unit(g, h, 0), unit(g, h, -1), unit(g, h, 1)
                    hn = (h + 1) % H
                    if h == H - 1 and group(g + 1):
                        wait(act, pe_vv, H * (g + 1))
                        nc.scalar.copy(x1h[:, :, :], x1f[:, :, bass.ds((g + 1) * GT, GT)]).then_inc(act_x1, 1)
                    if h == 1 and group(g - 1):
                        wait(act, pe_y, H * g)
                        for b in range(GB):
                            last = nc.scalar.activation(yg[:, 0, b * T:(b + 1) * T], Yb[0][:, b * T:(b + 1) * T],
                                                        ACT.Identity, bias=gb1[:, 0, bass.ds((g - 1) * GB + b, 1)],
                                                        scale=ada[:, 4, bass.ds((g - 1) * GB + b, 1)])
                        last.then_inc(act_y, 1)
                    if n is not None:
                        wait(act, dve_mx, n + 1)
                        wait(act, pe_pt, n - 1)
                        for b in range(GB):
                            last = nc.scalar.activation(probs[:, h % 2, b, :], Sb[:, b * T:(b + 1) * T], ACT.Exp,
                                                        bias=nm[:, h % 2, b:b + 1],
                                                        accum_out=sums[:, h % 2, b:b + 1])
                        last.then_inc(act_ex, 1)
                    if prev is not None:
                        wait(act, pe_o, prev + 1)
                        nc.scalar.activation(oh[:, :], Ob[:, :], ACT.Identity,
                                             bias=qkvb[:, 2, (h - 1) % H:(h - 1) % H + 1]).then_inc(act_oh, 1)
                    if nxt is not None:
                        wait(act, pe_q, nxt + 1)
                        nc.scalar.activation(Q[:, hn % 2, :], Qb[:, :], ACT.Identity, bias=qb_s[:, hn:hn + 1],
                                             scale=SC).then_inc(act_q, 1)
                        wait(act, pe_k, nxt + 1)
                        nc.scalar.activation(K[:, hn % 2, :], Kb[:, :], ACT.Identity,
                                             bias=qkvb[:, 1, hn:hn + 1]).then_inc(act_k, 1)

                run(act, step)

            @block.vector
            def _(dve):
                def step(g, h):
                    n, prev, nxt = unit(g, h, 0), unit(g, h, -1), unit(g, h, 1)
                    hn = (h + 1) % H
                    if h == H - 1 and group(g + 1):
                        wait(dve, act_x1, g + 2)
                        dve.tensor_tensor(x1l[:, :, :], x1f[:, :, bass.ds((g + 1) * GT, GT)],
                                          x1h[:, :, :].bitcast(F32), ALU.subtract).then_inc(dve_x1, 1)
                    if prev is not None:
                        wait(dve, pe_pt, prev + 1)
                        dve.tensor_copy(pT[:, :], Tb[:, :]).then_inc(dve_pt, 1)
                    if h == 1 and group(g - 1):
                        wait(dve, pe_y, H * g)
                        for b in range(GB):
                            last = dve.tensor_scalar(yg[:, 1, b * T:(b + 1) * T], Yb[1][:, b * T:(b + 1) * T],
                                                     ada[:, 5, bass.ds((g - 1) * GB + b, 1)],
                                                     gb1[:, 1, bass.ds((g - 1) * GB + b, 1)], ALU.mult, ALU.add)
                        last.then_inc(dve_y, 1)
                    if n is not None:
                        wait(dve, pe_sc, n + 1)
                        dve.tensor_reduce(nm[:, h % 2, :], Sb[:, :].rearrange("p (b k) -> p b k", b=GB), AX_X,
                                          ALU.max, negate=True).then_inc(dve_mx, 1)
                        wait(dve, act_ex, n + 1)
                        dve.reciprocal(rinv[:, h % 2, :], sums[:, h % 2, :]).then_inc(dve_ri, 1)
                    if prev is not None:
                        wait(dve, act_oh, prev + 1)
                        dve.scalar_tensor_tensor(ol[:, :], Ob[:, :], qkvb[:, 2, (h - 1) % H:(h - 1) % H + 1],
                                                 oh[:, :].bitcast(F32), ALU.add, ALU.subtract).then_inc(dve_ol, 1)
                    if h in (2, 3) and group(g - 1):
                        wait(dve, pe_yt, 2 * g + h - 3)
                        if h == 2:
                            dve.wait_ge(saved, 16)
                        xg = X[:, bass.ds((g - 1) * GB + 2 * (h - 2), 2), :]
                        dve.tensor_tensor(xg, Tb[:, :].rearrange("p (b d) -> p b d", b=2), xg,
                                          ALU.add).then_inc(dve_xa, 1)
                    if nxt is not None:
                        wait(dve, pe_vv, nxt + 1)
                        dve.tensor_copy(V[:, hn // 2 % 2, 2 * (hn % 2):2 * (hn % 2) + 2, :],
                                        Vb[:, :].rearrange("p (b d) -> p b d", b=2)).then_inc(dve_v, 1)

                run(dve, step)

            @block.gpsimd
            def _(pool):
                def step(g, h):
                    n = unit(g, h, 0)
                    if n is not None:
                        wait(pool, dve_ri, n + 1)
                        pool.tensor_tensor(probs[:, h % 2, :, :], probs[:, h % 2, :, :],
                                           rinv[:, h % 2, :, None].to_broadcast([P, GB, T]),
                                           ALU.mult).then_inc(pool_p, 1)

                run(pool, step)


def ffn(nc, sem, sb, kept, x2f, X, w_hi, w_lo, ada, gb2, b1, ident, banks, out):
    UN = NG * MC
    Hb, Yb, Tb = banks[0:2], banks[2:4], banks[4:6]
    x2 = [w[:, X2_COL:X2_COL + KT * B * T].rearrange("p (k t) -> p k t", k=KT) for w in (w_hi, w_lo)]
    hid = [w[:, HID_COL:HID_COL + 4 * GT].rearrange("p (s t) -> p s t", s=4) for w in (w_hi, w_lo)]
    with ExitStack() as ctx:
        hf = sb(ctx, "hf", [P, 2, GT])
        yg = sb(ctx, "yg2", [P, KT, GT])
        xk = sb(ctx, "xk", [P, B, DIM])
        l_xk = sem("l_xk")
        act_x2, dve_x2, pe_f1, act_g, act_hh, dve_hl, pe_f2, act_y2, dve_y2, pe_y2t, dve_xo, stored = (
            sem(n) for n in ("act_x2", "dve_x2", "pe_f1", "act_g", "act_hh", "dve_hl", "pe_f2", "act_y2", "dve_y2",
                             "pe_y2t", "dve_xo", "stored"))

        def run(eng, step):
            for c in range(MC - 2, MC):
                step(-1, c)
            for c in range(MC):
                step(0, c)
            with eng.Fori(1, NG - 1) as g:
                for c in range(MC):
                    step(g, c)
            for c in range(MC):
                step(NG - 1, c)
            for c in range(2):
                step(NG, c)

        def unit(g, c, ahead):
            u = g * MC + c + ahead
            if isinstance(u, int) and not 0 <= u < UN:
                return None
            return u

        def group(g):
            return not isinstance(g, int) or 0 <= g < NG

        with nc.Block() as block:

            @block.tensor
            def _(pe):
                def step(g, c):
                    m, nxt = unit(g, c, 0), unit(g, c, 2)
                    cn = (c + 2) % MC
                    gn = g + (c + 2) // MC
                    if nxt is not None:
                        if cn == 0:
                            wait(pe, dve_x2, gn + 1)
                        wait(pe, act_g, nxt - 1)
                        products(nc, Hb[c % 2][:, :],
                                 lambda k: w_hi[:, k * MLP + cn * P:k * MLP + (cn + 1) * P],
                                 lambda k: w_lo[:, k * MLP + cn * P:k * MLP + (cn + 1) * P],
                                 lambda k: x2[0][:, k, bass.ds(gn * GT, GT)],
                                 lambda k: x2[1][:, k, bass.ds(gn * GT, GT)],
                                 True, True, range(KT)).then_inc(pe_f1, 1)
                    if m is not None:
                        wait(pe, dve_hl, m + 1)
                        if c == 0:
                            wait(pe, act_y2, g)
                            wait(pe, dve_y2, g)
                        for d in range(KT):
                            c0 = KT * MLP + c * DIM + d * P
                            last = products(nc, Yb[d][:, :], lambda k: w_hi[:, c0:c0 + P],
                                            lambda k: w_lo[:, c0:c0 + P], lambda k: hid[0][:, c % 4, :],
                                            lambda k: hid[1][:, c % 4, :], c == 0, c == MC - 1, range(1))
                        last.then_inc(pe_f2, 1)
                    if c == 1 and group(g - 1):
                        wait(pe, act_y2, g)
                        wait(pe, dve_y2, g)
                        for b in range(GB):
                            for d in range(KT):
                                last = nc.tensor.transpose(
                                    Tb[b // 2][:, b % 2 * DIM + d * P:b % 2 * DIM + (d + 1) * P],
                                    yg[:, d, b * T:(b + 1) * T], ident)
                        last.then_inc(pe_y2t, 1)

                run(pe, step)

            @block.scalar
            def _(act):
                def split(g):
                    nc.scalar.copy(x2[0][:, :, bass.ds(g * GT, GT)], x2f[:, :, bass.ds(g * GT, GT)]
                                   ).then_inc(act_x2, 1)

                def step(g, c):
                    if c == 0 and group(g - 1):
                        wait(act, pe_f2, MC * g)
                        for b in range(GB):
                            last = nc.scalar.activation(yg[:, 0, b * T:(b + 1) * T], Yb[0][:, b * T:(b + 1) * T],
                                                        ACT.Identity, bias=gb2[:, 0, bass.ds((g - 1) * GB + b, 1)],
                                                        scale=ada[:, 10, bass.ds((g - 1) * GB + b, 1)])
                        last.then_inc(act_y2, 1)
                    nxt = unit(g, c, 2)
                    if nxt is not None:
                        cn = (c + 2) % MC
                        wait(act, pe_f1, nxt + 1)
                        wait(act, dve_hl, nxt - 1)
                        nc.scalar.activation(hf[:, c % 2, :], Hb[c % 2][:, :], ACT.Gelu,
                                             bias=b1[:, cn:cn + 1]).then_inc(act_g, 1)
                        wait(act, act_g, nxt + 1)
                        nc.scalar.copy(hid[0][:, cn % 4, :], hf[:, c % 2, :]).then_inc(act_hh, 1)
                    if c == 3 and group(g + 1):
                        split(g + 1)

                split(0)
                run(act, step)

            @block.vector
            def _(dve):
                def split(g):
                    wait(dve, act_x2, g + 1)
                    dve.tensor_tensor(x2[1][:, :, bass.ds(g * GT, GT)], x2f[:, :, bass.ds(g * GT, GT)],
                                      x2[0][:, :, bass.ds(g * GT, GT)].bitcast(F32),
                                      ALU.subtract).then_inc(dve_x2, 1)

                def step(g, c):
                    if c == 0 and group(g - 1):
                        wait(dve, pe_f2, MC * g)
                        for b in range(GB):
                            last = dve.tensor_scalar(yg[:, 1, b * T:(b + 1) * T], Yb[1][:, b * T:(b + 1) * T],
                                                     ada[:, 11, bass.ds((g - 1) * GB + b, 1)],
                                                     gb2[:, 1, bass.ds((g - 1) * GB + b, 1)], ALU.mult, ALU.add)
                        last.then_inc(dve_y2, 1)
                    nxt = unit(g, c, 2)
                    if nxt is not None:
                        cn = (c + 2) % MC
                        wait(dve, act_hh, nxt + 1)
                        dve.tensor_tensor(hid[1][:, cn % 4, :], hf[:, c % 2, :], hid[0][:, cn % 4, :].bitcast(F32),
                                          ALU.subtract).then_inc(dve_hl, 1)
                    if c == 1 and group(g - 1):
                        wait(dve, pe_y2t, g)
                        for i in range(2):
                            xg = X[:, bass.ds((g - 1) * GB + 2 * i, 2), :]
                            last = dve.tensor_tensor(xg, Tb[i][:, :].rearrange("p (b d) -> p b d", b=2), xg, ALU.add)
                        last.then_inc(dve_xo, 1)
                    if c == 3 and group(g + 1):
                        split(g + 1)
                    if c == 5 and group(g):
                        dve.wait_ge(l_xk, 16)
                        xg = X[:, bass.ds(g * GB, GB), :]
                        dve.tensor_tensor(xg, xk[:, bass.ds(g * GB, GB), :], xg, ALU.add)

                split(0)
                run(dve, step)

            @block.sync
            def _(sp):
                sp.dma_start(xk[:, :, :], kept.rearrange("b p d -> p b d")).then_inc(l_xk, 16)
                for g in range(NG):
                    sp.wait_ge(dve_xo, g + 1)
                    sp.dma_start(out[g * GB:(g + 1) * GB].rearrange("b p d -> p b d"),
                                 X[:, g * GB:(g + 1) * GB, :]).then_inc(stored, 16)
                sp.wait_ge(stored, 16 * NG)


_INS = ["x", "cond_2048", "L0_cond_Wq", "L0_cond_Wo", "L1_cond_ada_w", "L1_cond_ada_b", "L1_cond_qkv_w",
        "L1_cond_qkv_b", "L1_cond_out_w", "L1_cond_out_b", "L1_cond_ffn_w1", "L1_cond_ffn_b1", "L1_cond_ffn_w2",
        "L1_cond_ffn_b2"]


def constants(np):
    c = np.zeros((P, C_ID + P), np.float32)
    c[:, C_ID:] = np.eye(P, dtype=np.float32)
    c[:, C_RA] = c[:, C_CA] = 1.0
    for r in (0, 64):
        c[r + DK:r + 2 * DK, C_AQ] = -1.0
        c[r + 2 * DK:r + 3 * DK, C_AK] = -1.0
        one = r + ROWS_ONE
        c[one:one + 2, C_BH] = c[one:one + 2, C_AQ] = c[one:one + 2, C_AK] = 1.0
        c[one, C_CA], c[one, C_CB] = -NEG * DK ** 0.5, NEG * DK ** 0.5
        c[one + 1, C_RA], c[one + 1, C_CA], c[one + 1, C_CB] = 0.0, 0.0, 1.0
    return c


def kernel(**inputs):
    import numpy as _np
    import concourse.bacc as _bacc
    from concourse import mybir as _mybir
    from concourse.bass_utils import run_bass_kernel_spmd as _run

    nc = _bacc.Bacc("TRN2", target_bir_lowering=False, num_devices=1)
    arrays, args = {}, []
    for name in _INS:
        a = _np.ascontiguousarray(inputs[name])
        arrays[f"in_{name}_dram"] = a
        args.append(nc.dram_tensor(f"in_{name}_dram", a.shape, _mybir.dt.from_np(a.dtype), kind="ExternalInput").ap())
    arrays["stack_constants"] = constants(_np)
    args.append(nc.dram_tensor("stack_constants", (P, C_ID + P), F32, kind="ExternalInput").ap())
    out = nc.dram_tensor("out_dram", (B, T, DIM), F32, kind="ExternalOutput").ap()
    build(nc, *args, out)
    r = _run(nc, [arrays], core_ids=[0])
    return r.results[0]["out_dram"]
```

```python
from contextlib import ExitStack

import concourse.bass as bass
from concourse import mybir

ALU = mybir.AluOpType
ACT = mybir.ActivationFunctionType
F32 = mybir.dt.float32
F32R = mybir.dt.float32r
I32 = mybir.dt.int32
AX_X = mybir.AxisListType.X

P = 128
B, T, DIM = 16, 128, 256
NH, DK = 8, 16
UNITS = B // 2 * 4
NEG = -1e30
H, DH = 16, 128
KT = DIM // P
INNER = H * DH
MLP = 4 * DIM
MC = MLP // P
GB = 4
NG = B // GB
GT = GB * T
HP = 32
ROWS_ONE = 48
EPS = 1e-6
QKV_COLS = KT * 3 * INNER
W_COLS = QKV_COLS + H * DIM
CHUNK = 1024
SC = DH ** -0.5
FFN_COLS = KT * MLP + MC * DIM
X2_COL = FFN_COLS
HID_COL = X2_COL + KT * B * T
C_AQ, C_AK, C_BH, C_RA, C_RB, C_CA, C_CB, C_ID = 0, 1, 2, 3, 4, 5, 6, 8


def wait(eng, sem, value):
    if not isinstance(value, int) or value > 0:
        eng.wait_ge(sem, value)


def build(nc, x, cond, Wq, Wo, ada_w, ada_b, qkv_w, qkv_b, out_w, out_b, ffn_w1, ffn_b1, ffn_w2, ffn_b2, consts, out):
    top = ExitStack()

    def sem(name):
        return top.enter_context(nc.semaphore(name))

    def sb(ctx, name, shape, dt=F32):
        return ctx.enter_context(nc.sbuf_tensor(name, shape, dt))

    with top:
        X = sb(top, "X", [P, B, DIM])
        w_hi = sb(top, "w_hi", [P, W_COLS], F32R)
        w_lo = sb(top, "w_lo", [P, W_COLS], F32R)
        cst = sb(top, "cst", [P, C_ID + P])
        ada = sb(top, "ada", [P, 12, B])
        gb1 = sb(top, "gb1", [P, KT, B])
        gb2 = sb(top, "gb2", [P, KT, B])
        qkvb = sb(top, "qkvb", [P, 3, H])
        qb_s = sb(top, "qb_s", [P, H])
        adab = sb(top, "adab", [P, 12])
        ob = sb(top, "ob", [P, KT])
        b1 = sb(top, "b1", [P, MC])
        b2 = sb(top, "b2", [P, KT])
        ident = cst[:, C_ID:C_ID + P]
        psum = [top.enter_context(nc.psum_tensor(f"bank{i}", [P, 512], F32)) for i in range(4)]
        ring = top.enter_context(nc.psum_tensor("ring", [P, 4, 512], F32))
        banks = psum + [ring[:, i, :] for i in range(4)]

        first_block(nc, sem, sb, x, cond, Wq, Wo, ada_w, ada_b, qkv_w, qkv_b, out_w, out_b, ffn_b1, ffn_b2,
                    consts, X, w_hi, w_lo, cst, ada, gb1, gb2, qkvb, qb_s, adab, ob, b1, b2, ident, psum, ring)
        kept = nc.dram_tensor("kept", (B, T, DIM), F32).ap()
        saved = sem("saved")
        with ExitStack() as ctx:
            x1f = sb(ctx, "x1f", [P, KT, B * T])
            layernorm(nc, sem, sb, "one", X, ada, 2, 0, ident, banks, x1f, save=(kept, saved))
            attention(nc, sem, sb, saved, x1f, X, w_hi, w_lo, ada, gb1, qkvb, qb_s, ident, banks)
        with ExitStack() as ctx:
            x2f = sb(ctx, "x2f", [P, KT, B * T])
            raw = sb(ctx, "raw", [P, FFN_COLS])
            layernorm(nc, sem, sb, "two", X, ada, 8, 6, ident, banks, x2f,
                      ffn_weights=(ffn_w1, ffn_w2, raw, w_hi, w_lo))
            ffn(nc, sem, sb, kept, x2f, X, w_hi, w_lo, ada, gb2, b1, ident, banks, out)


def first_block(nc, sem, sb, x, cond, Wq, Wo, ada_w, ada_b, qkv_w, qkv_b, out_w, out_b, ffn_b1, ffn_b2,
                consts, X, w_hi, w_lo, cst, ada, gb1, gb2, qkvb, qb_s, adab, ob, b1, b2, ident, psum, ring):
    vbank, tbank, O = psum[0], psum[1], [psum[2], psum[3]]
    with ExitStack() as ctx:
        wqoT = sb(ctx, "wqoT", [P, 2, P])
        wst = sb(ctx, "wst", [P, 4, P])
        cndT = sb(ctx, "cndT", [P, KT, B])
        mb = sb(ctx, "mb", [P, 512])
        R = sb(ctx, "R", [P, 512])
        C = sb(ctx, "C", [P, 512])
        xs = sb(ctx, "xs", [P, 512])
        hs = sb(ctx, "hs", [P, 512], F32R)
        qst = sb(ctx, "qst", [P, 4, 512], F32R)
        kst = sb(ctx, "kst", [P, 4, 512], F32R)
        qst2 = sb(ctx, "qst2", [P, 512], F32R)
        mcol = sb(ctx, "mcol", [P, 4, P], F32R)
        identr = sb(ctx, "identr", [P, P], F32R)
        pt = sb(ctx, "pt", [P, 2, 1024])
        V = sb(ctx, "V", [P, 4, NH, HP])
        oT = sb(ctx, "oT", [P, 2, 512])
        rin = sb(ctx, "rin", [P, 2, 2 * NH])
        ctxs = sb(ctx, "ctxs", [P, 4, P])
        ctxT = sb(ctx, "ctxT", [P, 512])
        wqo = ctxs[:, 0:2, :]
        cnd = ctxs[0:B, 2:4, :].rearrange("p a n -> p (a n)")
        stage = sb(ctx, "stage", [P, 2, CHUNK])

        l_cst = sem("l_cst")
        l_small, l_w, l_x0, l_x, l_ada, l_mb, l_xs = (sem(n) for n in (
            "l_small", "l_w", "l_x0", "l_x", "l_ada", "l_mb", "l_xs"))
        l_st = [sem("l_st0"), sem("l_st1")]
        act_ident = sem("act_ident")
        pe_wT, wT_done, pe_ada, ada_done, set_done, wst_done, pool_set = (sem(n) for n in (
            "pe_wT", "wT_done", "pe_ada", "ada_done", "set_done", "wst_done", "pool_set"))
        pe_proj, act_h, dve_st, pool_st, pe_s, dve_max, pe_t, dve_q2, pe_st, act_exp, pe_pv = (sem(n) for n in (
            "pe_proj", "act_h", "dve_st", "pool_st", "pe_s", "dve_max", "pe_t", "dve_q2", "pe_st", "act_exp", "pe_pv"))
        pe_v, act_v, dve_rin, dve_ctx, pe_ctxT, act_ctxT, pe_out, dve_x, act_rc, act_hi, pool_lo, act_o, pe_oT = (sem(n) for n in (
            "pe_v", "act_v", "dve_rin", "dve_ctx", "pe_ctxT", "act_ctxT", "pe_out", "dve_x", "act_rc", "act_hi",
            "pool_lo", "act_o", "pe_oT"))

        qkv_v = qkv_w.rearrange("(k p) n -> p k n", p=P)
        outw_v = out_w.rearrange("(h p) n -> p h n", p=P)
        NGR = UNITS // 4

        def run(eng, step):
            for n in range(-4, 4):
                step(n // 4, n % 4)
            with eng.Fori(1, NGR - 2) as g:
                for t in range(4):
                    step(g, t)
            for n in range(UNITS - 8, UNITS + 4):
                step(n // 4, n % 4)

        def unit(g, t, ahead):
            u = g * 4 + t + ahead
            if isinstance(u, int) and not 0 <= u < UNITS:
                return None, None
            return u, (t + ahead) % 4

        def pair(g):
            return not isinstance(g, int) or 0 <= g < NGR

        with nc.Block() as block:

            @block.sync
            def _(sp):
                sp.dma_start(cst[:, :], consts).then_inc(l_cst, 16)
                sp.dma_start(wqo[:, 0, :], Wq).then_inc(l_w, 16)
                sp.dma_start(wqo[:, 1, :], Wo).then_inc(l_w, 16)
                sp.dma_start(cnd, cond).then_inc(l_w, 16)
                sp.dma_start(X[:, 0:2, :], x[0:2].rearrange("b p d -> p b d")).then_inc(l_x0, 16)

                def mask(g):
                    wait(sp, act_rc, g)
                    src = cond[2 * g:2 * g + 2, :].rearrange("b d -> (b d)").partition_broadcast(P)
                    sp.dma_start(mb[:, :], src).then_inc(l_mb, 16)

                def statics(g):
                    wait(sp, pe_v, g)
                    sp.dma_start(xs[:, :].rearrange("p (b d) -> p b d", b=2),
                                 x[2 * g:2 * g + 2].rearrange("b p d -> p b d")).then_inc(l_xs, 16)

                mask(0)
                statics(0)
                sp.dma_start(pt[:, :, :].rearrange("p a n -> p (a n)")[:, 0:6 * DIM], ada_w[0:P, :]).then_inc(l_ada, 16)
                sp.dma_start(stage[:, :, :].rearrange("p a n -> p (a n)")[:, 0:6 * DIM],
                             ada_w[P:2 * P, :]).then_inc(l_ada, 16)
                sp.dma_start(X[:, 2:B, :], x[2:B].rearrange("b p d -> p b d")).then_inc(l_x, 16)
                for dst, src, n in ((adab, ada_b, 12), (ob, out_b, KT), (b1, ffn_b1, MC), (b2, ffn_b2, KT)):
                    sp.dma_start(dst[:, :], src.rearrange("(n p) -> p n", p=P),
                                 allow_slow_non_contiguous=True).then_inc(l_small, 16)
                sp.dma_start(qkvb[:, :, :], qkv_b.rearrange("(s h p) -> p s h", s=3, p=P),
                             allow_slow_non_contiguous=True).then_inc(l_small, 16)
                for c in range(W_COLS // CHUNK):
                    if c < 2:
                        sp.wait_ge(ada_done, 1)
                    else:
                        sp.wait_ge(pool_lo, 2 * (c - 1))
                    if c < QKV_COLS // CHUNK:
                        k, n = divmod(c, 3 * INNER // CHUNK)
                        src = qkv_v[:, k, n * CHUNK:(n + 1) * CHUNK]
                        dst = stage[:, c % 2, :]
                    else:
                        n = c - QKV_COLS // CHUNK
                        src = outw_v[:, n * 4:n * 4 + 4, :]
                        dst = stage[:, c % 2, :].rearrange("p (h n) -> p h n", h=4)
                    if c % 2 == 0 and c // 2 + 1 < NGR:
                        mask(c // 2 + 1)
                    sp.dma_start(dst, src).then_inc(l_st[c % 2], 16)
                    if c % 2 == 1 and c // 2 + 1 < NGR:
                        statics(c // 2 + 1)

            @block.gpsimd
            def _(pool):
                pool.memset(mcol[:, :, :].bitcast(F32), 0.0)
                pool.memset(wst[:, :, :], 0.0)
                pool.memset(V[:, :, :, DK + 1:HP], 0.0)
                pool.memset(V[:, :, :, DK:DK + 1], 1.0).then_inc(pool_set, 1)

                def step(g, t):
                    u, j = unit(g, t, 4)
                    if u is not None:
                        if t == 0:
                            wait(pool, act_rc, g + 2)
                        wait(pool, dve_st, u + 1)
                        pool.tensor_tensor(qst[:, j, :], qst[:, j, :].bitcast(F32), R[:, :], ALU.mult)
                        pool.tensor_tensor(kst[:, j, :], kst[:, j, :].bitcast(F32), C[:, :],
                                           ALU.mult).then_inc(pool_st, 1)
                    n, _ = unit(g, t, 0)
                    if n is not None:
                        wait(pool, act_hi, n + 1)
                        cols = bass.ds(n * 512, 512)
                        pool.tensor_tensor(w_lo[:, cols], stage[:, t // 2, t % 2 * 512:t % 2 * 512 + 512],
                                           w_hi[:, cols].bitcast(F32), ALU.subtract).then_inc(pool_lo, 1)

                run(pool, step)

            @block.tensor
            def _(pe):
                pe.wait_ge(l_cst, 16)
                pe.wait_ge(l_w, 48)
                for i in range(2):
                    nc.tensor.transpose(tbank[:, i * P:(i + 1) * P], wqo[:, i, :], ident)
                for k in range(KT):
                    last = nc.tensor.transpose(tbank[:, 256 + k * B:256 + (k + 1) * B], cnd[:, k * P:(k + 1) * P],
                                               ident[0:B, 0:B])
                last.then_inc(pe_wT, 1)
                pe.wait_ge(wT_done, 1)
                pe.wait_ge(l_ada, 32)
                aw = [pt[:, :, :].rearrange("p a n -> p (a n)"), stage[:, :, :].rearrange("p a n -> p (a n)")]
                for m in range(12):
                    for k in range(KT):
                        last = nc.tensor.matmul(vbank[:, m * B:(m + 1) * B], aw[k][:, m * P:(m + 1) * P],
                                                cndT[:, k, :], start=(k == 0), stop=(k == KT - 1))
                last.then_inc(pe_ada, 1)
                pe.wait_ge(ada_done, 1)
                pe.wait_ge(wst_done, 1)
                pe.wait_ge(pool_set, 1)
                pe.wait_ge(act_ident, 1)
                pe.wait_ge(l_x0, 16)

                def values(g):
                    wait(pe, l_xs, 16 * (g + 1))
                    for bk in range(4):
                        last = nc.tensor.matmul(tbank[:, bk * P:(bk + 1) * P], xs[:, bk * P:(bk + 1) * P],
                                                wqoT[:, 0, :], start=True, stop=True)
                    last.then_inc(pe_v, 1)

                def pv(n, j, b):
                    for s in range(2):
                        r0, half = divmod(2 * j + s, 4)[::-1]
                        for kt in range(2):
                            last = nc.tensor.matmul(O[b][r0 * HP:(r0 + 1) * HP, half * 256:half * 256 + 256],
                                                    V[:, b * 2 + kt, 2 * j + s, :],
                                                    pt[:, b, (s * 2 + kt) * 256:(s * 2 + kt + 1) * 256],
                                                    start=(kt == 0), stop=(kt == 1))
                    last.then_inc(pe_pv, 1)

                def scores(u, ju, b):
                    wait(pe, dve_max, 2 * u + b)
                    for qt in range(2):
                        for s in range(2):
                            r = slice(64 * s, 64 * s + 64)
                            q0 = b * 256 + qt * P
                            last = nc.tensor.matmul(ring[:, s, qt * 256:qt * 256 + 256], qst[r, ju, q0:q0 + P],
                                                    kst[r, ju, b * 256:b * 256 + 256], start=True, stop=True)
                    last.then_inc(pe_s, 1)

                def shifted(u, ju, b):
                    wait(pe, act_exp, 2 * u + b)
                    for kt in range(2):
                        for s in range(2):
                            r = slice(64 * s, 64 * s + 64)
                            k0 = b * 256 + kt * P
                            last = nc.tensor.matmul(ring[:, 2 + s, kt * 256:kt * 256 + 256], kst[r, ju, k0:k0 + P],
                                                    qst2[r, b * 256:b * 256 + 256], start=True, stop=True)
                    last.then_inc(pe_st, 1)

                def step(g, t):
                    n, j = unit(g, t, 0)
                    u1, j1 = unit(g, t, 1)
                    u2, j2 = unit(g, t, 2)
                    u4, j4 = unit(g, t, 4)
                    if u1 is not None:
                        wait(pe, dve_max, 2 * u1 + 2)
                        if t == 0:
                            wait(pe, act_v, g + 1)
                        elif t < 3 and pair(g - 1):
                            wait(pe, dve_ctx, 2 * g + t - 2)
                        elif pair(g - 1):
                            wait(pe, act_ctxT, g)
                        for i in range(4):
                            last = nc.tensor.matmul(tbank[:, i * P:(i + 1) * P], mcol[:, i, :], identr[:, :],
                                                    start=True, stop=True)
                        last.then_inc(pe_t, 1)
                    if u2 is not None:
                        wait(pe, pool_st, u2 + 1)
                        scores(u2, j2, 0)
                    if u4 is not None:
                        wait(pe, dve_st, u4)
                        if isinstance(u4, int) and u4 == 4:
                            pe.wait_ge(l_x, 16)
                        nc.tensor.matmul(vbank[:, :].rearrange("p (b d) -> p b d", b=2), wst[:, j4, :],
                                         X[:, bass.ds(g * 2 + 2, 2), :], start=True, stop=True).then_inc(pe_proj, 1)
                    if n is not None:
                        if t == 0:
                            wait(pe, act_v, g + 1)
                            wait(pe, act_o, 2 * g - 1)
                        wait(pe, act_exp, 2 * n + 1)
                        pv(n, j, 0)
                    if u1 is not None:
                        wait(pe, dve_q2, u1 + 1)
                        shifted(u1, j1, 0)
                    if t < 2 and pair(g - 1):
                        wait(pe, act_o, 2 * g + t - 1)
                        if u1 is None:
                            wait(pe, *((dve_x, g - 1), (dve_ctx, 2 * g - 1))[t])
                        for half in range(2):
                            for qt in range(2):
                                last = nc.tensor.transpose(tbank[:, (2 * qt + half) * P:(2 * qt + half + 1) * P],
                                                           oT[:, t, (2 * half + qt) * P:(2 * half + qt + 1) * P], ident)
                        last.then_inc(pe_oT, 1)
                    if t == 2 and pair(g - 1):
                        wait(pe, dve_ctx, 2 * g)
                        for i in range(4):
                            last = nc.tensor.transpose(tbank[:, i * P:(i + 1) * P], ctxs[:, i, :], ident)
                        last.then_inc(pe_ctxT, 1)
                    if t == 3 and pair(g - 1):
                        wait(pe, act_ctxT, g)
                        nc.tensor.matmul(tbank[:, :], wqoT[:, 1, :], ctxT[:, :], start=True,
                                         stop=True).then_inc(pe_out, 1)
                    if u2 is not None:
                        scores(u2, j2, 1)
                    if n is not None:
                        wait(pe, act_exp, 2 * n + 2)
                        if t == 0:
                            wait(pe, act_o, 2 * g)
                        pv(n, j, 1)
                    if t == 3 and pair(g + 1):
                        if pair(g - 1):
                            wait(pe, dve_x, g)
                        values(g + 1)
                    if u1 is not None:
                        shifted(u1, j1, 1)

                run(pe, step)

            @block.scalar
            def _(act):
                act.wait_ge(l_cst, 16)
                nc.scalar.copy(identr[:, :], ident).then_inc(act_ident, 1)

                def sums(g, b):
                    wait(act, pe_pv, 8 * g + 7 + b)
                    nc.scalar.copy(oT[:, b, :], O[b][:, :]).then_inc(act_o, 1)

                def step(g, t):
                    n, _ = unit(g, t, 0)
                    u, _ = unit(g, t, 1)
                    u4, _ = unit(g, t, 4)
                    if u4 is not None:
                        wait(act, pe_proj, u4 + 1)
                        nc.scalar.activation(hs[:, :], vbank[:, :], ACT.Identity,
                                             bias=cst[:, C_BH:C_BH + 1]).then_inc(act_h, 1)
                    if t == 0 and pair(g + 1):
                        wait(act, pool_st, 4 * g + 4)
                        wait(act, l_mb, 16 * (g + 2))
                        nc.scalar.activation(R[:, :], mb[:, :], ACT.Identity, bias=cst[:, C_RB:C_RB + 1],
                                             scale=cst[:, C_RA:C_RA + 1])
                        nc.scalar.activation(C[:, :], mb[:, :], ACT.Identity, bias=cst[:, C_CB:C_CB + 1],
                                             scale=cst[:, C_CA:C_CA + 1]).then_inc(act_rc, 1)

                    def exponentials(b):
                        wait(act, pe_st, 2 * u + b + 1)
                        wait(act, pe_pv, 2 * (u - 1) + b + 1)
                        nc.scalar.activation(pt[:, b, :], ring[:, 2:4, :], ACT.Exp,
                                             scale=DK ** -0.5).then_inc(act_exp, 1)

                    if u is not None:
                        exponentials(0)
                    if t == 2 and pair(g - 1):
                        wait(act, pe_ctxT, g)
                        nc.scalar.copy(ctxT[:, :], tbank[:, :]).then_inc(act_ctxT, 1)
                    if t == 3 and pair(g):
                        sums(g, 0)
                    if n is not None:
                        wait(act, l_st[t // 2], 16 * (g + 1))
                        nc.scalar.copy(w_hi[:, bass.ds(n * 512, 512)],
                                       stage[:, t // 2, t % 2 * 512:t % 2 * 512 + 512]).then_inc(act_hi, 1)
                    if t == 3 and pair(g + 1):
                        wait(act, pe_v, g + 2)
                        if isinstance(g, int) and g == -1:
                            act.wait_ge(pool_set, 1)
                        nc.scalar.copy(V[:, :, :, 0:DK],
                                       tbank[:, :].rearrange("p (k h d) -> p k h d", k=4, h=NH)).then_inc(act_v, 1)
                    if t == 3 and pair(g):
                        sums(g, 1)
                    if u is not None:
                        exponentials(1)

                run(act, step)

            @block.vector
            def _(dve):
                count = [0]

                def chain(ins):
                    count[0] += 1
                    ins.then_inc(set_done, 1)
                    dve.wait_ge(set_done, count[0])

                dve.wait_ge(pe_wT, 1)
                chain(dve.tensor_copy(wqoT[:, :, :], tbank[:, 0:256].rearrange("p (i n) -> p i n", i=2)))
                dve.tensor_copy(cndT[:, :, :], tbank[:, 256:256 + KT * B].rearrange("p (k n) -> p k n", k=KT)
                                ).then_inc(wT_done, 1)
                dve.wait_ge(pool_set, 1)
                wv = wst[:, :, :].rearrange("p j (s e d) -> p (j s) e d", s=2, d=DK)
                for slot in range(3):
                    last = dve.tensor_copy(wv[:, :, slot, :], wqoT[:, 0, :].rearrange("p (h d) -> p h d", h=NH))
                last.then_inc(wst_done, 1)
                dve.wait_ge(pe_ada, 1)
                dve.wait_ge(l_small, 80)
                chain(dve.tensor_tensor(ada[:, :, :], vbank[:, 0:12 * B].rearrange("p (m b) -> p m b", m=12),
                                        adab[:, :, None].to_broadcast([P, 12, B]), ALU.add))
                chain(dve.tensor_scalar(ada[:, 2:4, :], ada[:, 2:4, :], 1.0, None, ALU.add))
                chain(dve.tensor_scalar(ada[:, 8:10, :], ada[:, 8:10, :], 1.0, None, ALU.add))
                chain(dve.tensor_tensor(gb1[:, :, :], ada[:, 4:6, :], ob[:, :, None].to_broadcast([P, KT, B]), ALU.mult))
                chain(dve.tensor_tensor(gb2[:, :, :], ada[:, 10:12, :], b2[:, :, None].to_broadcast([P, KT, B]),
                                        ALU.mult))
                dve.tensor_scalar(qb_s[:, :], qkvb[:, 0, :], SC, None, ALU.mult).then_inc(ada_done, 1)

                def step(g, t):
                    u, ju = unit(g, t, 1)
                    if u is not None:
                        wait(dve, pe_t, u + 1)
                        dve.tensor_tensor(qst2[:, :], tbank[:, :], qst[:, ju, :].bitcast(F32),
                                          ALU.add).then_inc(dve_q2, 1)
                    u2, _ = unit(g, t, 2)

                    def maxima(b):
                        wait(dve, pe_s, 2 * u2 + b + 1)
                        dst = mcol[:, 2 * b:2 * b + 2, :].rearrange("p q (s r) -> p s q r", s=2)[
                            :, :, :, ROWS_ONE + 1]
                        src = ring[:, 0:2, :].rearrange("p s (q k) -> p s q k", q=2)
                        dve.tensor_reduce(dst, src, AX_X, ALU.max, negate=True).then_inc(dve_max, 1)

                    if u2 is not None:
                        maxima(0)
                    u, ju = unit(g, t, 4)
                    if u is not None:
                        wait(dve, act_h, u + 1)
                        h = hs[:, :].bitcast(F32)
                        dve.scalar_tensor_tensor(qst[:, ju, :], h, cst[:, C_AQ:C_AQ + 1], vbank[:, :],
                                                 ALU.mult, ALU.add)
                        dve.scalar_tensor_tensor(kst[:, ju, :], h, cst[:, C_AK:C_AK + 1], vbank[:, :],
                                                 ALU.mult, ALU.add).then_inc(dve_st, 1)
                    if t < 2 and pair(g - 1):
                        wait(dve, pe_oT, 2 * g + t - 1)
                        ov = tbank[:, :].rearrange("p (h d) -> p h d", d=HP)
                        dve.reciprocal(rin[:, t, :], ov[:, :, DK]).then_inc(dve_rin, 1)
                        wait(dve, dve_rin, 2 * g + t - 1)
                        dve.tensor_tensor(ctxs[:, 2 * t:2 * t + 2, :].rearrange("p q (h d) -> p (q h) d", d=DK),
                                          ov[:, :, 0:DK], rin[:, t, :, None].to_broadcast([P, 2 * NH, DK]),
                                          ALU.mult).then_inc(dve_ctx, 1)
                    if t == 3 and pair(g - 1):
                        wait(dve, pe_out, g)
                        xg = X[:, bass.ds(g * 2 - 2, 2), :]
                        dve.tensor_tensor(xg, tbank[:, :].rearrange("p (b d) -> p b d", b=2), xg,
                                          ALU.add).then_inc(dve_x, 1)
                    if u2 is not None:
                        maxima(1)

                run(dve, step)



def layernorm(nc, sem, sb, tag, X, ada, scale0, shift0, ident, banks, xf, ffn_weights=None, save=None):
    with ExitStack() as ctx:
        xn = sb(ctx, f"xn_{tag}", [P, B, DIM])
        bst = sb(ctx, f"bst_{tag}", [P, B, 6])
        mv = sb(ctx, f"mv_{tag}", [P, B, 2])
        ve = sb(ctx, f"ve_{tag}", [P, B])
        rst = sb(ctx, f"rst_{tag}", [P, B])
        nwt = sb(ctx, f"nwt_{tag}", [P, B])
        chained, dve_xn, pe_xt, act_m, dve_m, l_raw, act_whi, pool_wlo = (sem(f"{n}_{tag}") for n in (
            "chained", "dve_xn", "pe_xt", "act_m", "dve_m", "l_raw", "act_whi", "pool_wlo"))
        with nc.Block() as block:

            if save:
                @block.sync
                def _(sp):
                    sp.dma_start(save[0].rearrange("b p d -> p b d"), X[:, :, :]).then_inc(save[1], 16)

            if ffn_weights:
                w1, w2, raw, w_hi, w_lo = ffn_weights

                @block.sync
                def _(sp):
                    sp.dma_start(raw[:, 0:KT * MLP].rearrange("p (k n) -> p k n", k=KT),
                                 w1.rearrange("(k p) n -> p k n", p=P)).then_inc(l_raw, 16)
                    sp.dma_start(raw[:, KT * MLP:FFN_COLS].rearrange("p (c n) -> p c n", c=MC),
                                 w2.rearrange("(c p) n -> p c n", p=P)).then_inc(l_raw, 16)

                @block.gpsimd
                def _(pool):
                    for i in range(2):
                        cols = slice(i * KT * MLP, (i + 1) * KT * MLP)
                        pool.wait_ge(act_whi, i + 1)
                        pool.tensor_tensor(w_lo[:, cols], raw[:, cols], w_hi[:, cols].bitcast(F32),
                                           ALU.subtract).then_inc(pool_wlo, 1)

            @block.tensor
            def _(pe):
                for g in range(NG):
                    for b in range(GB):
                        pe.wait_ge(dve_xn, g * GB + b + 1)
                        for k in range(KT):
                            last = nc.tensor.transpose(banks[2 * g + k][:, b * T:(b + 1) * T],
                                                       xn[:, g * GB + b, k * P:(k + 1) * P], ident)
                    last.then_inc(pe_xt, 1)

            @block.scalar
            def _(act):
                if ffn_weights:
                    act.wait_ge(l_raw, 32)
                    for i in range(2):
                        cols = slice(i * KT * MLP, (i + 1) * KT * MLP)
                        nc.scalar.copy(w_hi[:, cols], raw[:, cols]).then_inc(act_whi, 1)
                for g in range(NG):
                    act.wait_ge(pe_xt, g + 1)
                    for b in range(GB * g, GB * g + GB):
                        last = nc.scalar.activation(xf[:, 0, b * T:(b + 1) * T],
                                                    banks[2 * g][:, (b - GB * g) * T:(b - GB * g + 1) * T],
                                                    ACT.Identity, bias=ada[:, shift0, b:b + 1],
                                                    scale=ada[:, scale0, b:b + 1])
                    last.then_inc(act_m, 1)

            @block.vector
            def _(dve):
                count = [0]

                def chain(ins):
                    count[0] += 1
                    ins.then_inc(chained, 1)
                    dve.wait_ge(chained, count[0])

                for b in range(B):
                    last = dve.bn_stats(bst[:, b, :], X[:, b, :])
                chain(last)
                for b in range(B):
                    last = dve.bn_aggr(mv[:, b, :], bst[:, b, :])
                chain(last)
                chain(dve.tensor_scalar(ve[:, :], mv[:, :, 1], EPS, None, ALU.add))
                chain(dve.tensor_scalar(rst[:, :].bitcast(I32), ve[:, :].bitcast(I32), -0.5, 1597463007.0,
                                        ALU.mult, ALU.add))
                for _ in range(4):
                    chain(dve.tensor_tensor(nwt[:, :], rst[:, :], rst[:, :], ALU.mult))
                    chain(dve.tensor_tensor(nwt[:, :], nwt[:, :], ve[:, :], ALU.mult))
                    chain(dve.tensor_scalar(nwt[:, :], nwt[:, :], -0.5, 1.5, ALU.mult, ALU.add))
                    chain(dve.tensor_tensor(rst[:, :], rst[:, :], nwt[:, :], ALU.mult))

                def modulate(g):
                    dve.wait_ge(pe_xt, g + 1)
                    for b in range(GB * g, GB * g + GB):
                        last = dve.tensor_scalar(xf[:, 1, b * T:(b + 1) * T],
                                                 banks[2 * g + 1][:, (b - GB * g) * T:(b - GB * g + 1) * T],
                                                 ada[:, scale0 + 1, b:b + 1], ada[:, shift0 + 1, b:b + 1],
                                                 ALU.mult, ALU.add)
                    last.then_inc(dve_m, 1)

                for g in range(NG):
                    for b in range(GB * g, GB * g + GB):
                        dve.tensor_scalar(xn[:, b, :], X[:, b, :], mv[:, b, 0:1], rst[:, b:b + 1],
                                          ALU.subtract, ALU.mult).then_inc(dve_xn, 1)
                    if g:
                        modulate(g - 1)
                modulate(NG - 1)


def products(nc, bank, w_hi, w_lo, x_hi, x_lo, start, stop, ks):
    terms = [(w, x, k) for k in ks for w, x in ((w_hi, x_hi), (w_hi, x_lo), (w_lo, x_hi))]
    for i, (w, x, k) in enumerate(terms):
        last = nc.tensor.matmul(bank, w(k), x(k), start=(start and i == 0), stop=(stop and i == len(terms) - 1))
    return last


def attention(nc, sem, sb, saved, x1f, X, w_hi, w_lo, ada, gb1, qkvb, qb_s, ident, banks):
    UN = NG * H
    Qb, Kb, Vb, Sb, Tb, Ob = banks[0:6]
    Yb = banks[6:8]
    with ExitStack() as ctx:
        x1h = sb(ctx, "x1h", [P, KT, GT], F32R)
        x1l = sb(ctx, "x1l", [P, KT, GT], F32R)
        Q = sb(ctx, "Q", [P, 2, GT])
        K = sb(ctx, "K", [P, 2, GT])
        V = sb(ctx, "Vv", [P, 2, GB, 2 * DH])
        probs = sb(ctx, "probs", [P, 2, GB, T])
        pT = sb(ctx, "pT", [P, GT])
        oh = sb(ctx, "oh", [P, GT], F32R)
        ol = sb(ctx, "ol", [P, GT], F32R)
        yg = sb(ctx, "yg", [P, KT, GT])
        nm = sb(ctx, "nm", [P, 2, GB])
        sums = sb(ctx, "sums", [P, 2, GB])
        rinv = sb(ctx, "rinv", [P, 2, GB])
        (act_x1, dve_x1, pe_q, act_q, pe_k, act_k, pe_vv, dve_v, pe_sc, dve_mx, act_ex, dve_ri, pool_p, pe_pt, dve_pt,
         pe_o, act_oh, dve_ol, pe_y, act_y, dve_y, pe_yt, dve_xa) = (sem(n) for n in (
             "act_x1", "dve_x1", "pe_q", "act_q", "pe_k", "act_k", "pe_vv", "dve_v", "pe_sc", "dve_mx", "act_ex",
             "dve_ri", "pool_p", "pe_pt", "dve_pt", "pe_o", "act_oh", "dve_ol", "pe_y", "act_y", "dve_y", "pe_yt",
             "dve_xa"))

        def run(eng, step):
            step(-1, H - 1)
            for h in range(H):
                step(0, h)
            with eng.Fori(1, NG - 1) as g:
                for h in range(H):
                    step(g, h)
            for h in range(H):
                step(NG - 1, h)
            for h in range(4):
                step(NG, h)

        def unit(g, h, ahead):
            u = g * H + h + ahead
            if isinstance(u, int) and not 0 <= u < UN:
                return None
            return u

        def group(g):
            return not isinstance(g, int) or 0 <= g < NG

        with nc.Block() as block:

            @block.tensor
            def _(pe):
                def project(bank, part, hd):
                    def w(t):
                        return lambda k: t[:, k * 3 * INNER + part * INNER + hd * DH:
                                           k * 3 * INNER + part * INNER + (hd + 1) * DH]
                    return products(nc, bank[:, :], w(w_hi), w(w_lo), lambda k: x1h[:, k, :], lambda k: x1l[:, k, :],
                                    True, True, range(KT))

                def step(g, h):
                    n, prev, nxt = unit(g, h, 0), unit(g, h, -1), unit(g, h, 1)
                    hn = (h + 1) % H
                    if prev is not None:
                        wait(pe, pool_p, prev + 1)
                        wait(pe, dve_pt, prev)
                        if h in (3, 4) and group(g - 1):
                            wait(pe, dve_xa, 2 * g + h - 4)
                        for b in range(GB):
                            last = nc.tensor.transpose(Tb[:, b * T:(b + 1) * T], probs[:, (h + 1) % 2, b, :], ident)
                        last.then_inc(pe_pt, 1)
                    if n is not None:
                        wait(pe, act_q, n + 1)
                        wait(pe, act_k, n + 1)
                        wait(pe, act_ex, n)
                        for b in range(GB):
                            t = slice(b * T, (b + 1) * T)
                            last = nc.tensor.matmul(Sb[:, t], Q[:, h % 2, t], K[:, h % 2, t], start=True, stop=True)
                        last.then_inc(pe_sc, 1)
                    if nxt is not None:
                        if hn == 0:
                            wait(pe, dve_x1, g + 2)
                        project(Qb, 0, hn).then_inc(pe_q, 1)
                    if prev is not None:
                        wait(pe, dve_pt, prev + 1)
                        wait(pe, dve_v, prev + (2 if h % 2 else 1))
                        wait(pe, dve_ol, prev)
                        for b in range(GB):
                            last = nc.tensor.matmul(Ob[:, b * T:(b + 1) * T],
                                                    V[:, (h - 1) % H // 2 % 2, b, (h + 1) % 2 * DH:
                                                      ((h + 1) % 2 + 1) * DH],
                                                    pT[:, b * T:(b + 1) * T], start=True, stop=True)
                        last.then_inc(pe_o, 1)
                    if h in (2, 3) and group(g - 1):
                        wait(pe, act_y, g)
                        wait(pe, dve_y, g)
                        if h == 3:
                            wait(pe, dve_xa, 2 * g - 1)
                        for b in range(2):
                            for d in range(KT):
                                t0 = (2 * (h - 2) + b) * T
                                last = nc.tensor.transpose(Tb[:, b * DIM + d * P:b * DIM + (d + 1) * P],
                                                           yg[:, d, t0:t0 + T], ident)
                        last.then_inc(pe_yt, 1)
                    if nxt is not None:
                        project(Kb, 1, hn).then_inc(pe_k, 1)
                        wait(pe, dve_v, nxt)
                        for i in range(2):
                            b = 2 * (hn % 2) + i
                            c0 = 2 * INNER + hn // 2 * 2 * DH
                            last = products(nc, Vb[:, i * 2 * DH:(i + 1) * 2 * DH],
                                            lambda k: x1h[:, k, b * T:(b + 1) * T],
                                            lambda k: x1l[:, k, b * T:(b + 1) * T],
                                            lambda k: w_hi[:, k * 3 * INNER + c0:k * 3 * INNER + c0 + 2 * DH],
                                            lambda k: w_lo[:, k * 3 * INNER + c0:k * 3 * INNER + c0 + 2 * DH],
                                            True, True, range(KT))
                        last.then_inc(pe_vv, 1)
                    if prev is not None:
                        hp = (h - 1) % H
                        wait(pe, dve_ol, prev + 1)
                        if hp == 0:
                            wait(pe, act_y, g)
                            wait(pe, dve_y, g)
                        for d in range(KT):
                            c = QKV_COLS + hp * DIM + d * P
                            last = products(nc, Yb[d][:, :], lambda k: w_hi[:, c:c + P], lambda k: w_lo[:, c:c + P],
                                            lambda k: oh[:, :], lambda k: ol[:, :], hp == 0, hp == H - 1, range(1))
                        last.then_inc(pe_y, 1)

                run(pe, step)

            @block.scalar
            def _(act):
                def step(g, h):
                    n, prev, nxt = unit(g, h, 0), unit(g, h, -1), unit(g, h, 1)
                    hn = (h + 1) % H
                    if h == H - 1 and group(g + 1):
                        wait(act, pe_vv, H * (g + 1))
                        nc.scalar.copy(x1h[:, :, :], x1f[:, :, bass.ds((g + 1) * GT, GT)]).then_inc(act_x1, 1)
                    if h == 1 and group(g - 1):
                        wait(act, pe_y, H * g)
                        for b in range(GB):
                            last = nc.scalar.activation(yg[:, 0, b * T:(b + 1) * T], Yb[0][:, b * T:(b + 1) * T],
                                                        ACT.Identity, bias=gb1[:, 0, bass.ds((g - 1) * GB + b, 1)],
                                                        scale=ada[:, 4, bass.ds((g - 1) * GB + b, 1)])
                        last.then_inc(act_y, 1)
                    if n is not None:
                        wait(act, dve_mx, n + 1)
                        wait(act, pe_pt, n - 1)
                        for b in range(GB):
                            last = nc.scalar.activation(probs[:, h % 2, b, :], Sb[:, b * T:(b + 1) * T], ACT.Exp,
                                                        bias=nm[:, h % 2, b:b + 1],
                                                        accum_out=sums[:, h % 2, b:b + 1])
                        last.then_inc(act_ex, 1)
                    if prev is not None:
                        wait(act, pe_o, prev + 1)
                        nc.scalar.activation(oh[:, :], Ob[:, :], ACT.Identity,
                                             bias=qkvb[:, 2, (h - 1) % H:(h - 1) % H + 1]).then_inc(act_oh, 1)
                    if nxt is not None:
                        wait(act, pe_q, nxt + 1)
                        nc.scalar.activation(Q[:, hn % 2, :], Qb[:, :], ACT.Identity, bias=qb_s[:, hn:hn + 1],
                                             scale=SC).then_inc(act_q, 1)
                        wait(act, pe_k, nxt + 1)
                        nc.scalar.activation(K[:, hn % 2, :], Kb[:, :], ACT.Identity,
                                             bias=qkvb[:, 1, hn:hn + 1]).then_inc(act_k, 1)

                run(act, step)

            @block.vector
            def _(dve):
                def step(g, h):
                    n, prev, nxt = unit(g, h, 0), unit(g, h, -1), unit(g, h, 1)
                    hn = (h + 1) % H
                    if h == H - 1 and group(g + 1):
                        wait(dve, act_x1, g + 2)
                        dve.tensor_tensor(x1l[:, :, :], x1f[:, :, bass.ds((g + 1) * GT, GT)],
                                          x1h[:, :, :].bitcast(F32), ALU.subtract).then_inc(dve_x1, 1)
                    if prev is not None:
                        wait(dve, pe_pt, prev + 1)
                        dve.tensor_copy(pT[:, :], Tb[:, :]).then_inc(dve_pt, 1)
                    if h == 1 and group(g - 1):
                        wait(dve, pe_y, H * g)
                        for b in range(GB):
                            last = dve.tensor_scalar(yg[:, 1, b * T:(b + 1) * T], Yb[1][:, b * T:(b + 1) * T],
                                                     ada[:, 5, bass.ds((g - 1) * GB + b, 1)],
                                                     gb1[:, 1, bass.ds((g - 1) * GB + b, 1)], ALU.mult, ALU.add)
                        last.then_inc(dve_y, 1)
                    if n is not None:
                        wait(dve, pe_sc, n + 1)
                        dve.tensor_reduce(nm[:, h % 2, :], Sb[:, :].rearrange("p (b k) -> p b k", b=GB), AX_X,
                                          ALU.max, negate=True).then_inc(dve_mx, 1)
                        wait(dve, act_ex, n + 1)
                        dve.reciprocal(rinv[:, h % 2, :], sums[:, h % 2, :]).then_inc(dve_ri, 1)
                    if prev is not None:
                        wait(dve, act_oh, prev + 1)
                        dve.scalar_tensor_tensor(ol[:, :], Ob[:, :], qkvb[:, 2, (h - 1) % H:(h - 1) % H + 1],
                                                 oh[:, :].bitcast(F32), ALU.add, ALU.subtract).then_inc(dve_ol, 1)
                    if h in (2, 3) and group(g - 1):
                        wait(dve, pe_yt, 2 * g + h - 3)
                        if h == 2:
                            dve.wait_ge(saved, 16)
                        xg = X[:, bass.ds((g - 1) * GB + 2 * (h - 2), 2), :]
                        dve.tensor_tensor(xg, Tb[:, :].rearrange("p (b d) -> p b d", b=2), xg,
                                          ALU.add).then_inc(dve_xa, 1)
                    if nxt is not None:
                        wait(dve, pe_vv, nxt + 1)
                        dve.tensor_copy(V[:, hn // 2 % 2, 2 * (hn % 2):2 * (hn % 2) + 2, :],
                                        Vb[:, :].rearrange("p (b d) -> p b d", b=2)).then_inc(dve_v, 1)

                run(dve, step)

            @block.gpsimd
            def _(pool):
                def step(g, h):
                    n = unit(g, h, 0)
                    if n is not None:
                        wait(pool, dve_ri, n + 1)
                        pool.tensor_tensor(probs[:, h % 2, :, :], probs[:, h % 2, :, :],
                                           rinv[:, h % 2, :, None].to_broadcast([P, GB, T]),
                                           ALU.mult).then_inc(pool_p, 1)

                run(pool, step)


def ffn(nc, sem, sb, kept, x2f, X, w_hi, w_lo, ada, gb2, b1, ident, banks, out):
    UN = NG * MC
    Hb, Yb, Tb = banks[0:2], banks[2:4], banks[4:6]
    x2 = [w[:, X2_COL:X2_COL + KT * B * T].rearrange("p (k t) -> p k t", k=KT) for w in (w_hi, w_lo)]
    hid = [w[:, HID_COL:HID_COL + 4 * GT].rearrange("p (s t) -> p s t", s=4) for w in (w_hi, w_lo)]
    with ExitStack() as ctx:
        hf = sb(ctx, "hf", [P, 2, GT])
        yg = sb(ctx, "yg2", [P, KT, GT])
        xk = sb(ctx, "xk", [P, B, DIM])
        l_xk = sem("l_xk")
        act_x2, dve_x2, pe_f1, act_g, act_hh, dve_hl, pe_f2, act_y2, dve_y2, pe_y2t, dve_xo, stored = (
            sem(n) for n in ("act_x2", "dve_x2", "pe_f1", "act_g", "act_hh", "dve_hl", "pe_f2", "act_y2", "dve_y2",
                             "pe_y2t", "dve_xo", "stored"))

        def run(eng, step):
            for c in range(MC - 2, MC):
                step(-1, c)
            for c in range(MC):
                step(0, c)
            with eng.Fori(1, NG - 1) as g:
                for c in range(MC):
                    step(g, c)
            for c in range(MC):
                step(NG - 1, c)
            for c in range(2):
                step(NG, c)

        def unit(g, c, ahead):
            u = g * MC + c + ahead
            if isinstance(u, int) and not 0 <= u < UN:
                return None
            return u

        def group(g):
            return not isinstance(g, int) or 0 <= g < NG

        with nc.Block() as block:

            @block.tensor
            def _(pe):
                def step(g, c):
                    m, nxt = unit(g, c, 0), unit(g, c, 2)
                    cn = (c + 2) % MC
                    gn = g + (c + 2) // MC
                    if nxt is not None:
                        if cn == 0:
                            wait(pe, dve_x2, gn + 1)
                        wait(pe, act_g, nxt - 1)
                        products(nc, Hb[c % 2][:, :],
                                 lambda k: w_hi[:, k * MLP + cn * P:k * MLP + (cn + 1) * P],
                                 lambda k: w_lo[:, k * MLP + cn * P:k * MLP + (cn + 1) * P],
                                 lambda k: x2[0][:, k, bass.ds(gn * GT, GT)],
                                 lambda k: x2[1][:, k, bass.ds(gn * GT, GT)],
                                 True, True, range(KT)).then_inc(pe_f1, 1)
                    if m is not None:
                        wait(pe, dve_hl, m + 1)
                        if c == 0:
                            wait(pe, act_y2, g)
                            wait(pe, dve_y2, g)
                        for d in range(KT):
                            c0 = KT * MLP + c * DIM + d * P
                            last = products(nc, Yb[d][:, :], lambda k: w_hi[:, c0:c0 + P],
                                            lambda k: w_lo[:, c0:c0 + P], lambda k: hid[0][:, c % 4, :],
                                            lambda k: hid[1][:, c % 4, :], c == 0, c == MC - 1, range(1))
                        last.then_inc(pe_f2, 1)
                    if c == 1 and group(g - 1):
                        wait(pe, act_y2, g)
                        wait(pe, dve_y2, g)
                        for b in range(GB):
                            for d in range(KT):
                                last = nc.tensor.transpose(
                                    Tb[b // 2][:, b % 2 * DIM + d * P:b % 2 * DIM + (d + 1) * P],
                                    yg[:, d, b * T:(b + 1) * T], ident)
                        last.then_inc(pe_y2t, 1)

                run(pe, step)

            @block.scalar
            def _(act):
                def split(g):
                    nc.scalar.copy(x2[0][:, :, bass.ds(g * GT, GT)], x2f[:, :, bass.ds(g * GT, GT)]
                                   ).then_inc(act_x2, 1)

                def step(g, c):
                    if c == 0 and group(g - 1):
                        wait(act, pe_f2, MC * g)
                        for b in range(GB):
                            last = nc.scalar.activation(yg[:, 0, b * T:(b + 1) * T], Yb[0][:, b * T:(b + 1) * T],
                                                        ACT.Identity, bias=gb2[:, 0, bass.ds((g - 1) * GB + b, 1)],
                                                        scale=ada[:, 10, bass.ds((g - 1) * GB + b, 1)])
                        last.then_inc(act_y2, 1)
                    nxt = unit(g, c, 2)
                    if nxt is not None:
                        cn = (c + 2) % MC
                        wait(act, pe_f1, nxt + 1)
                        wait(act, dve_hl, nxt - 1)
                        nc.scalar.activation(hf[:, c % 2, :], Hb[c % 2][:, :], ACT.Gelu,
                                             bias=b1[:, cn:cn + 1]).then_inc(act_g, 1)
                        wait(act, act_g, nxt + 1)
                        nc.scalar.copy(hid[0][:, cn % 4, :], hf[:, c % 2, :]).then_inc(act_hh, 1)
                    if c == 3 and group(g + 1):
                        split(g + 1)

                split(0)
                run(act, step)

            @block.vector
            def _(dve):
                def split(g):
                    wait(dve, act_x2, g + 1)
                    dve.tensor_tensor(x2[1][:, :, bass.ds(g * GT, GT)], x2f[:, :, bass.ds(g * GT, GT)],
                                      x2[0][:, :, bass.ds(g * GT, GT)].bitcast(F32),
                                      ALU.subtract).then_inc(dve_x2, 1)

                def step(g, c):
                    if c == 0 and group(g - 1):
                        wait(dve, pe_f2, MC * g)
                        for b in range(GB):
                            last = dve.tensor_scalar(yg[:, 1, b * T:(b + 1) * T], Yb[1][:, b * T:(b + 1) * T],
                                                     ada[:, 11, bass.ds((g - 1) * GB + b, 1)],
                                                     gb2[:, 1, bass.ds((g - 1) * GB + b, 1)], ALU.mult, ALU.add)
                        last.then_inc(dve_y2, 1)
                    nxt = unit(g, c, 2)
                    if nxt is not None:
                        cn = (c + 2) % MC
                        wait(dve, act_hh, nxt + 1)
                        dve.tensor_tensor(hid[1][:, cn % 4, :], hf[:, c % 2, :], hid[0][:, cn % 4, :].bitcast(F32),
                                          ALU.subtract).then_inc(dve_hl, 1)
                    if c == 1 and group(g - 1):
                        wait(dve, pe_y2t, g)
                        for i in range(2):
                            xg = X[:, bass.ds((g - 1) * GB + 2 * i, 2), :]
                            last = dve.tensor_tensor(xg, Tb[i][:, :].rearrange("p (b d) -> p b d", b=2), xg, ALU.add)
                        last.then_inc(dve_xo, 1)
                    if c == 3 and group(g + 1):
                        split(g + 1)
                    if c == 5 and group(g):
                        dve.wait_ge(l_xk, 16)
                        xg = X[:, bass.ds(g * GB, GB), :]
                        dve.tensor_tensor(xg, xk[:, bass.ds(g * GB, GB), :], xg, ALU.add)

                split(0)
                run(dve, step)

            @block.sync
            def _(sp):
                sp.dma_start(xk[:, :, :], kept.rearrange("b p d -> p b d")).then_inc(l_xk, 16)
                for g in range(NG):
                    sp.wait_ge(dve_xo, g + 1)
                    sp.dma_start(out[g * GB:(g + 1) * GB].rearrange("b p d -> p b d"),
                                 X[:, g * GB:(g + 1) * GB, :]).then_inc(stored, 16)
                sp.wait_ge(stored, 16 * NG)


_INS = ["x", "cond_2048", "L0_cond_Wq", "L0_cond_Wo", "L1_cond_ada_w", "L1_cond_ada_b", "L1_cond_qkv_w",
        "L1_cond_qkv_b", "L1_cond_out_w", "L1_cond_out_b", "L1_cond_ffn_w1", "L1_cond_ffn_b1", "L1_cond_ffn_w2",
        "L1_cond_ffn_b2"]


def constants(np):
    c = np.zeros((P, C_ID + P), np.float32)
    c[:, C_ID:] = np.eye(P, dtype=np.float32)
    c[:, C_RA] = c[:, C_CA] = 1.0
    for r in (0, 64):
        c[r + DK:r + 2 * DK, C_AQ] = -1.0
        c[r + 2 * DK:r + 3 * DK, C_AK] = -1.0
        one = r + ROWS_ONE
        c[one:one + 2, C_BH] = c[one:one + 2, C_AQ] = c[one:one + 2, C_AK] = 1.0
        c[one, C_CA], c[one, C_CB] = -NEG * DK ** 0.5, NEG * DK ** 0.5
        c[one + 1, C_RA], c[one + 1, C_CA], c[one + 1, C_CB] = 0.0, 0.0, 1.0
    return c


def kernel(**inputs):
    import numpy as _np
    import concourse.bacc as _bacc
    from concourse import mybir as _mybir
    from concourse.bass_utils import run_bass_kernel_spmd as _run

    nc = _bacc.Bacc("TRN2", target_bir_lowering=False, num_devices=1)
    arrays, args = {}, []
    for name in _INS:
        a = _np.ascontiguousarray(inputs[name])
        arrays[f"in_{name}_dram"] = a
        args.append(nc.dram_tensor(f"in_{name}_dram", a.shape, _mybir.dt.from_np(a.dtype), kind="ExternalInput").ap())
    arrays["stack_constants"] = constants(_np)
    args.append(nc.dram_tensor("stack_constants", (P, C_ID + P), F32, kind="ExternalInput").ap())
    out = nc.dram_tensor("out_dram", (B, T, DIM), F32, kind="ExternalOutput").ap()
    build(nc, *args, out)
    r = _run(nc, [arrays], core_ids=[0])
    return r.results[0]["out_dram"]
```

```python
from contextlib import ExitStack

import concourse.bass as bass
from concourse import mybir

ALU = mybir.AluOpType
ACT = mybir.ActivationFunctionType
F32 = mybir.dt.float32
F32R = mybir.dt.float32r
I32 = mybir.dt.int32
AX_X = mybir.AxisListType.X

P = 128
B, T, DIM = 16, 128, 256
NH, DK = 8, 16
UNITS = B // 2 * 4
NEG = -1e30
H, DH = 16, 128
KT = DIM // P
INNER = H * DH
MLP = 4 * DIM
MC = MLP // P
GB = 4
NG = B // GB
GT = GB * T
HP = 32
ROWS_ONE = 48
EPS = 1e-6
QKV_COLS = KT * 3 * INNER
W_COLS = QKV_COLS + H * DIM
CHUNK = 1024
SC = DH ** -0.5
FFN_BLOCKS = [i * INNER for i in range(4)]
X2_COL = 4 * INNER
HID_COL = QKV_COLS
LINKS = 12
C_AQ, C_AK, C_BH, C_RA, C_RB, C_CA, C_CB, C_ID = 0, 1, 2, 3, 4, 5, 6, 8


def wait(eng, sem, value):
    if not isinstance(value, int) or value > 0:
        eng.wait_ge(sem, value)


def build(nc, x, cond, Wq, Wo, ada_w, ada_b, qkv_w, qkv_b, out_w, out_b, ffn_w1, ffn_b1, ffn_w2, ffn_b2, consts, out):
    top = ExitStack()

    def sem(name):
        return top.enter_context(nc.semaphore(name))

    def sb(ctx, name, shape, dt=F32):
        return ctx.enter_context(nc.sbuf_tensor(name, shape, dt))

    with top:
        X = sb(top, "X", [P, B, DIM])
        w_hi = sb(top, "w_hi", [P, W_COLS], F32R)
        w_lo = sb(top, "w_lo", [P, W_COLS], F32R)
        cst = sb(top, "cst", [P, C_ID + P])
        ada = sb(top, "ada", [P, 12, B])
        gb1 = sb(top, "gb1", [P, KT, B])
        gb2 = sb(top, "gb2", [P, KT, B])
        qkvb = sb(top, "qkvb", [P, 3, H])
        qb_s = sb(top, "qb_s", [P, H])
        adab = sb(top, "adab", [P, 12])
        ob = sb(top, "ob", [P, KT])
        b1 = sb(top, "b1", [P, MC])
        b2 = sb(top, "b2", [P, KT])
        ident = cst[:, C_ID:C_ID + P]
        psum = [top.enter_context(nc.psum_tensor(f"bank{i}", [P, 512], F32)) for i in range(4)]
        ring = top.enter_context(nc.psum_tensor("ring", [P, 4, 512], F32))
        banks = psum + [ring[:, i, :] for i in range(4)]

        norm1 = Norm(sem, sb, top, "one")
        dve_n1, pe_n1 = sem("dve_n1"), sem("pe_n1")
        first_block(nc, sem, sb, x, cond, Wq, Wo, ada_w, ada_b, qkv_w, qkv_b, out_w, out_b, ffn_b1, ffn_b2,
                    consts, X, w_hi, w_lo, cst, ada, gb1, gb2, qkvb, qb_s, adab, ob, b1, b2, ident, psum, ring,
                    norm1, dve_n1, pe_n1)
        kept = nc.dram_tensor("kept", (B, T, DIM), F32).ap()
        saved, act_x2, dve_x2, pe_f1 = (sem(n) for n in ("saved", "act_x2", "dve_x2", "pe_f1"))
        norm2 = Norm(sem, sb, top, "two")
        x2f = sb(top, "x2f", [P, KT, B * T])
        attention(nc, sem, sb, kept, saved, norm1, dve_n1, pe_n1, norm2, X, w_hi, w_lo, ada, gb1, qkvb, qb_s, ident,
                  banks, ffn_w1, ffn_w2, x2f, act_x2, dve_x2, pe_f1)
        ffn(nc, sem, sb, kept, norm2, x2f, act_x2, dve_x2, pe_f1, X, w_hi, w_lo, ada, gb2, b1, ident, banks, out)


class Norm:

    def __init__(self, sem, sb, ctx, tag):
        self.sums = sb(ctx, f"sums_{tag}", [P, GB])
        self.mean = sb(ctx, f"mean_{tag}", [P, GB])
        self.squares = sb(ctx, f"squares_{tag}", [P, GB])
        self.var = sb(ctx, f"var_{tag}", [P, GB])
        self.half = sb(ctx, f"half_{tag}", [P, GB])
        self.work = sb(ctx, f"work_{tag}", [P, GB])
        self.taken = sb(ctx, f"taken_{tag}", [P, 1])
        self.rst = sb(ctx, f"rst_{tag}", [P, GB])
        self.act_sums, self.act_squares = sem(f"act_sums_{tag}"), sem(f"act_squares_{tag}")
        self.linked = sem(f"linked_{tag}")


def transposed(nc, ident, xn, half, bank):
    for k in range(KT):
        for b in range(2):
            last = nc.tensor.transpose(bank[:, (2 * k + b) * P:(2 * k + b + 1) * P],
                                       xn(2 * half + b)[:, k * P:(k + 1) * P], ident)
    return last


def row_sums(nc, norm, X, g, junk):
    for b in range(GB):
        last = nc.scalar.activation(junk(b), X[:, bass.ds(g * GB + b, 1), :].rearrange("p o d -> p (o d)"), ACT.Identity,
                                    accum_out=norm.sums[:, b:b + 1])
    last.then_inc(norm.act_sums, 1)


def row_means(dve, norm, g):
    wait(dve, norm.act_sums, g + 1)
    dve.tensor_scalar(norm.mean[:, :], norm.sums[:, :], -1.0 / DIM, None, ALU.mult).then_inc(norm.linked, 1)


def row_squares(nc, act, norm, X, g, junk):
    wait(act, norm.linked, g * LINKS + 1)
    nc.scalar.copy(norm.taken[:, :], norm.mean[:, 0:1])
    for b in range(GB):
        last = nc.scalar.activation(junk(b), X[:, bass.ds(g * GB + b, 1), :].rearrange("p o d -> p (o d)"), ACT.Square,
                                    bias=norm.mean[:, b:b + 1], accum_out=norm.squares[:, b:b + 1])
    last.then_inc(norm.act_squares, 1)


def deviations(dve, norm, g):
    wait(dve, norm.act_squares, g + 1)
    dve.tensor_scalar(norm.var[:, :], norm.squares[:, :], 1.0 / DIM, EPS, ALU.mult, ALU.add).then_inc(norm.linked, 1)
    wait(dve, norm.linked, g * LINKS + 2)
    dve.tensor_scalar(norm.half[:, :], norm.var[:, :], -0.5, None, ALU.mult)
    dve.tensor_scalar(norm.rst[:, :].bitcast(I32), norm.var[:, :].bitcast(I32), -0.5, 1597463007.0,
                      ALU.mult, ALU.add).then_inc(norm.linked, 1)
    wait(dve, norm.linked, g * LINKS + 3)
    for i in range(3):
        dve.tensor_tensor(norm.work[:, :], norm.rst[:, :], norm.rst[:, :], ALU.mult).then_inc(norm.linked, 1)
        wait(dve, norm.linked, g * LINKS + 4 + 3 * i)
        dve.tensor_tensor(norm.work[:, :], norm.work[:, :], norm.half[:, :], ALU.mult).then_inc(norm.linked, 1)
        wait(dve, norm.linked, g * LINKS + 5 + 3 * i)
        dve.scalar_tensor_tensor(norm.rst[:, :], norm.work[:, :], 1.5, norm.rst[:, :], ALU.add,
                                 ALU.mult).then_inc(norm.linked, 1)
        wait(dve, norm.linked, g * LINKS + 6 + 3 * i)


def normal_rows(dve, norm, xn, X, g):
    for b in range(GB):
        last = dve.tensor_scalar(xn(b), X[:, bass.ds(g * GB + b, 1), :].rearrange("p o d -> p (o d)"),
                                 norm.mean[:, b:b + 1], norm.rst[:, b:b + 1], ALU.add, ALU.mult)
    return last


def first_block(nc, sem, sb, x, cond, Wq, Wo, ada_w, ada_b, qkv_w, qkv_b, out_w, out_b, ffn_b1, ffn_b2,
                consts, X, w_hi, w_lo, cst, ada, gb1, gb2, qkvb, qb_s, adab, ob, b1, b2, ident, psum, ring,
                norm1, dve_n1, pe_n1):
    vbank, tbank, O = psum[0], psum[1], [psum[2], psum[3]]
    with ExitStack() as ctx:
        wqoT = sb(ctx, "wqoT", [P, 2, P])
        wst = sb(ctx, "wst", [P, 4, P])
        mb = sb(ctx, "mb", [P, 512])
        R = sb(ctx, "R", [P, 512])
        C = sb(ctx, "C", [P, 512])
        xs = sb(ctx, "xs", [P, 512])
        hs = sb(ctx, "hs", [P, 512], F32R)
        qst = sb(ctx, "qst", [P, 4, 512], F32R)
        kst = sb(ctx, "kst", [P, 4, 512], F32R)
        qst2 = sb(ctx, "qst2", [P, 512], F32R)
        mcol = sb(ctx, "mcol", [P, 4, P], F32R)
        identr = sb(ctx, "identr", [P, P], F32R)
        pt = sb(ctx, "pt", [P, 2, 1024])
        V = sb(ctx, "V", [P, 4, NH, HP])
        oT = sb(ctx, "oT", [P, 2, 512])
        rin = sb(ctx, "rin", [P, 2, 2 * NH])
        ctxs = sb(ctx, "ctxs", [P, 4, P])
        ctxT = sb(ctx, "ctxT", [P, 512])
        wqo = ctxs[:, 0:2, :]
        cnd = ctxs[0:B, 2:4, :].rearrange("p a n -> p (a n)")
        cndT = ctxT[:, 0:KT * B].rearrange("p (k b) -> p k b", k=KT)
        stage = sb(ctx, "stage", [P, 2, CHUNK])

        l_cst = sem("l_cst")
        l_small, l_w, l_x0, l_x, l_ada, l_mb, l_xs = (sem(n) for n in (
            "l_small", "l_w", "l_x0", "l_x", "l_ada", "l_mb", "l_xs"))
        l_st = [sem("l_st0"), sem("l_st1")]
        act_ident = sem("act_ident")
        pe_wT, wT_done, pe_ada, ada_done, set_done, wst_done, pool_set = (sem(n) for n in (
            "pe_wT", "wT_done", "pe_ada", "ada_done", "set_done", "wst_done", "pool_set"))
        pe_proj, act_h, dve_st, pool_st, pe_s, dve_max, pe_t, dve_q2, pe_st, act_exp, pe_pv = (sem(n) for n in (
            "pe_proj", "act_h", "dve_st", "pool_st", "pe_s", "dve_max", "pe_t", "dve_q2", "pe_st", "act_exp", "pe_pv"))
        (pe_v, act_v, dve_rin, dve_ctx, pe_ctxT, act_ctxT, pe_out, dve_x, act_rc, act_hi, pool_lo, act_o,
         pe_oT) = (sem(n) for n in (
            "pe_v", "act_v", "dve_rin", "dve_ctx", "pe_ctxT", "act_ctxT", "pe_out", "dve_x", "act_rc", "act_hi",
            "pool_lo", "act_o", "pe_oT"))

        qkv_v = qkv_w.rearrange("(k p) n -> p k n", p=P)
        outw_v = out_w.rearrange("(h p) n -> p h n", p=P)

        def normal(b):
            return (R, C)[b // 2][:, b % 2 * DIM:(b % 2 + 1) * DIM]

        NGR = UNITS // 4

        def run(eng, step):
            for n in range(-5, 4):
                step(n // 4, n % 4)
            with eng.Fori(1, NGR - 2) as g:
                for t in range(4):
                    step(g, t)
            for n in range(UNITS - 8, UNITS + 4):
                step(n // 4, n % 4)

        def unit(g, t, ahead):
            u = g * 4 + t + ahead
            if isinstance(u, int) and not 0 <= u < UNITS:
                return None, None
            return u, (t + ahead) % 4

        def pair(g):
            return not isinstance(g, int) or 0 <= g < NGR

        with nc.Block() as block:

            @block.sync
            def _(sp):
                sp.dma_start(cst[:, :], consts).then_inc(l_cst, 16)
                sp.dma_start(wqo[:, 0, :], Wq).then_inc(l_w, 16)
                sp.dma_start(wqo[:, 1, :], Wo).then_inc(l_w, 16)
                sp.dma_start(cnd, cond).then_inc(l_w, 16)
                sp.dma_start(X[:, 0:2, :], x[0:2].rearrange("b p d -> p b d")).then_inc(l_x0, 16)

                def mask(g):
                    wait(sp, act_rc, g)
                    src = cond[2 * g:2 * g + 2, :].rearrange("b d -> (b d)").partition_broadcast(P)
                    sp.dma_start(mb[:, :], src).then_inc(l_mb, 16)

                def statics(g):
                    wait(sp, pe_v, g)
                    sp.dma_start(xs[:, :].rearrange("p (b d) -> p b d", b=2),
                                 x[2 * g:2 * g + 2].rearrange("b p d -> p b d")).then_inc(l_xs, 16)

                mask(0)
                statics(0)
                sp.dma_start(pt[:, :, :].rearrange("p a n -> p (a n)")[:, 0:6 * DIM], ada_w[0:P, :]).then_inc(l_ada, 16)
                sp.dma_start(stage[:, :, :].rearrange("p a n -> p (a n)")[:, 0:6 * DIM],
                             ada_w[P:2 * P, :]).then_inc(l_ada, 16)
                sp.dma_start(X[:, 2:B, :], x[2:B].rearrange("b p d -> p b d")).then_inc(l_x, 16)
                for dst, src, n in ((adab, ada_b, 12), (ob, out_b, KT), (b1, ffn_b1, MC), (b2, ffn_b2, KT)):
                    sp.dma_start(dst[:, :], src.rearrange("(n p) -> p n", p=P),
                                 allow_slow_non_contiguous=True).then_inc(l_small, 16)
                sp.dma_start(qkvb[:, :, :], qkv_b.rearrange("(s h p) -> p s h", s=3, p=P),
                             allow_slow_non_contiguous=True).then_inc(l_small, 16)
                for c in range(W_COLS // CHUNK):
                    if c < 2:
                        sp.wait_ge(pe_ada, 4)
                    else:
                        sp.wait_ge(pool_lo, 2 * (c - 1))
                    if c < QKV_COLS // CHUNK:
                        k, n = divmod(c, 3 * INNER // CHUNK)
                        src = qkv_v[:, k, n * CHUNK:(n + 1) * CHUNK]
                        dst = stage[:, c % 2, :]
                    else:
                        n = c - QKV_COLS // CHUNK
                        src = outw_v[:, n * 4:n * 4 + 4, :]
                        dst = stage[:, c % 2, :].rearrange("p (h n) -> p h n", h=4)
                    if c % 2 == 0 and c // 2 + 1 < NGR:
                        mask(c // 2 + 1)
                    sp.dma_start(dst, src).then_inc(l_st[c % 2], 16)
                    if c % 2 == 1 and c // 2 + 1 < NGR:
                        statics(c // 2 + 1)

            @block.gpsimd
            def _(pool):
                pool.memset(mcol[:, :, :].bitcast(F32), 0.0)
                pool.memset(wst[:, :, :], 0.0)
                pool.memset(V[:, :, :, DK + 1:HP], 0.0)
                pool.memset(V[:, :, :, DK:DK + 1], 1.0).then_inc(pool_set, 1)

                def step(g, t):
                    u, j = unit(g, t, 4)
                    if u is not None:
                        if t == 0:
                            wait(pool, act_rc, g + 2)
                        wait(pool, dve_st, u + 1)
                        pool.tensor_tensor(qst[:, j, :], qst[:, j, :].bitcast(F32), R[:, :], ALU.mult)
                        pool.tensor_tensor(kst[:, j, :], kst[:, j, :].bitcast(F32), C[:, :],
                                           ALU.mult).then_inc(pool_st, 1)
                    n, _ = unit(g, t, 0)
                    if n is not None:
                        wait(pool, act_hi, n + 1)
                        cols = bass.ds(n * 512, 512)
                        pool.tensor_tensor(w_lo[:, cols], stage[:, t // 2, t % 2 * 512:t % 2 * 512 + 512],
                                           w_hi[:, cols].bitcast(F32), ALU.subtract).then_inc(pool_lo, 1)

                run(pool, step)

            @block.tensor
            def _(pe):
                pe.wait_ge(l_cst, 16)
                pe.wait_ge(l_w, 48)
                for i in range(2):
                    nc.tensor.transpose(tbank[:, i * P:(i + 1) * P], wqo[:, i, :], ident)
                for k in range(KT):
                    last = nc.tensor.transpose(tbank[:, 256 + k * B:256 + (k + 1) * B], cnd[:, k * P:(k + 1) * P],
                                               ident[0:B, 0:B])
                last.then_inc(pe_wT, 1)

                def modulations(part):
                    if part == 0:
                        pe.wait_ge(l_ada, 32)
                    aw = [pt[:, :, :].rearrange("p a n -> p (a n)"), stage[:, :, :].rearrange("p a n -> p (a n)")]
                    for m in range(3 * part, 3 * part + 3):
                        for k in range(KT):
                            last = nc.tensor.matmul(O[1][:, m * B:(m + 1) * B], aw[k][:, m * P:(m + 1) * P],
                                                    cndT[:, k, :], start=(k == 0), stop=(k == KT - 1))
                    last.then_inc(pe_ada, 1)

                pe.wait_ge(wst_done, 1)
                pe.wait_ge(pool_set, 1)
                pe.wait_ge(act_ident, 1)
                pe.wait_ge(l_x0, 16)

                def values(g):
                    wait(pe, l_xs, 16 * (g + 1))
                    for bk in range(4):
                        last = nc.tensor.matmul(tbank[:, bk * P:(bk + 1) * P], xs[:, bk * P:(bk + 1) * P],
                                                wqoT[:, 0, :], start=True, stop=True)
                    last.then_inc(pe_v, 1)

                def pv(j):
                    for kt in range(2):
                        for b in range(2):
                            for s in range(2):
                                half, slot = divmod(2 * j + s, 4)
                                row = (slot + 2 * b) % 4 * HP
                                last = nc.tensor.matmul(O[b][row:row + HP, half * 256:half * 256 + 256],
                                                        V[:, b * 2 + kt, 2 * j + s, :],
                                                        pt[:, b, (s * 2 + kt) * 256:(s * 2 + kt + 1) * 256],
                                                        start=(kt == 0), stop=(kt == 1))
                    last.then_inc(pe_pv, 1)

                def scores(u, ju, b):
                    wait(pe, dve_max, 2 * u + b)
                    for qt in range(2):
                        for s in range(2):
                            r = slice(64 * s, 64 * s + 64)
                            q0 = b * 256 + qt * P
                            last = nc.tensor.matmul(ring[:, s, qt * 256:qt * 256 + 256], qst[r, ju, q0:q0 + P],
                                                    kst[r, ju, b * 256:b * 256 + 256], start=True, stop=True)
                    last.then_inc(pe_s, 1)

                def shifted(u, ju, b):
                    wait(pe, act_exp, 2 * u + b)
                    for kt in range(2):
                        for s in range(2):
                            r = slice(64 * s, 64 * s + 64)
                            k0 = b * 256 + kt * P
                            last = nc.tensor.matmul(ring[:, 2 + s, kt * 256:kt * 256 + 256], kst[r, ju, k0:k0 + P],
                                                    qst2[r, b * 256:b * 256 + 256], start=True, stop=True)
                    last.then_inc(pe_st, 1)

                def step(g, t):
                    n, j = unit(g, t, 0)
                    u1, j1 = unit(g, t, 1)
                    u2, j2 = unit(g, t, 2)
                    u5, j5 = unit(g, t, 5)
                    if isinstance(g, int) and g == -1 and t == 3:
                        modulations(3)
                    if u1 is not None:
                        wait(pe, dve_max, 2 * u1 + 2)
                        if t == 0:
                            wait(pe, act_v, g + 1)
                        elif t < 3 and pair(g - 1):
                            wait(pe, dve_ctx, 2 * g + t - 2)
                        elif pair(g - 1):
                            wait(pe, act_ctxT, g)
                        for i in range(4):
                            last = nc.tensor.matmul(tbank[:, i * P:(i + 1) * P], mcol[:, i, :], identr[:, :],
                                                    start=True, stop=True)
                        last.then_inc(pe_t, 1)
                    if u2 is not None:
                        wait(pe, pool_st, u2 + 1)
                        scores(u2, j2, 0)
                    if n is not None:
                        if t == 0:
                            wait(pe, act_v, g + 1)
                            wait(pe, act_o, 2 * g)
                            if isinstance(g, int) and g == 0:
                                pe.wait_ge(ada_done, 1)
                        wait(pe, act_exp, 2 * n + 2)
                        pv(j)
                    if u1 is not None:
                        wait(pe, dve_q2, u1 + 1)
                        shifted(u1, j1, 0)
                    if t < 2 and pair(g - 1):
                        wait(pe, act_o, 2 * g + t - 1)
                        if u1 is None:
                            wait(pe, *((dve_x, g - 1), (dve_ctx, 2 * g - 1))[t])
                        for half in range(2):
                            for qt in range(2):
                                last = nc.tensor.transpose(tbank[:, (2 * qt + half) * P:(2 * qt + half + 1) * P],
                                                           oT[:, t, (2 * half + qt) * P:(2 * half + qt + 1) * P], ident)
                        last.then_inc(pe_oT, 1)
                    if t == 2 and pair(g - 1):
                        wait(pe, dve_ctx, 2 * g)
                        for i in range(4):
                            last = nc.tensor.transpose(tbank[:, i * P:(i + 1) * P], ctxs[:, i, :], ident)
                        last.then_inc(pe_ctxT, 1)
                    if t == 3 and pair(g - 1):
                        wait(pe, act_ctxT, g)
                        nc.tensor.matmul(tbank[:, :], wqoT[:, 1, :], ctxT[:, :], start=True,
                                         stop=True).then_inc(pe_out, 1)
                    if u2 is not None:
                        scores(u2, j2, 1)
                    if t == 3 and pair(g + 1):
                        if pair(g - 1):
                            wait(pe, dve_x, g)
                        values(g + 1)
                    if u1 is not None:
                        shifted(u1, j1, 1)
                    if u5 is not None:
                        wait(pe, dve_st, u5)
                        if isinstance(u5, int) and u5 == 4:
                            pe.wait_ge(l_x, 16)
                        nc.tensor.matmul(vbank[:, :].rearrange("p (b d) -> p b d", b=2), wst[:, j5, :],
                                         X[:, bass.ds((g + (t + 5) // 4) * 2, 2), :], start=True,
                                         stop=True).then_inc(pe_proj, 1)
                    if isinstance(g, int) and g == -1 and t < 3:
                        modulations(t)
                    if isinstance(g, int) and g == NGR - 1 and t == 3:
                        pe.wait_ge(dve_n1, 1)
                        pe.wait_ge(dve_st, UNITS)
                        pe.wait_ge(dve_max, 2 * UNITS)
                        for half in range(2):
                            transposed(nc, ident, normal, half, (vbank, ring[:, 0, :])[half]).then_inc(pe_n1, 1)

                run(pe, step)

            @block.scalar
            def _(act):
                act.wait_ge(l_cst, 16)
                nc.scalar.copy(identr[:, :], ident).then_inc(act_ident, 1)

                def sums(g, b):
                    wait(act, pe_pv, 4 * g + 4)
                    nc.scalar.copy(oT[:, b, :], O[b][:, :]).then_inc(act_o, 1)

                def step(g, t):
                    n, _ = unit(g, t, 0)
                    u, _ = unit(g, t, 1)
                    u4, _ = unit(g, t, 4)
                    if u4 is not None:
                        wait(act, pe_proj, u4 + 1)
                        nc.scalar.activation(hs[:, :], vbank[:, :], ACT.Identity,
                                             bias=cst[:, C_BH:C_BH + 1]).then_inc(act_h, 1)
                    if t == 0 and pair(g + 1):
                        wait(act, pool_st, 4 * g + 4)
                        wait(act, l_mb, 16 * (g + 2))
                        nc.scalar.activation(R[:, :], mb[:, :], ACT.Identity, bias=cst[:, C_RB:C_RB + 1],
                                             scale=cst[:, C_RA:C_RA + 1])
                        nc.scalar.activation(C[:, :], mb[:, :], ACT.Identity, bias=cst[:, C_CB:C_CB + 1],
                                             scale=cst[:, C_CA:C_CA + 1]).then_inc(act_rc, 1)

                    def exponentials(b):
                        wait(act, pe_st, 2 * u + b + 1)
                        if isinstance(u, int) and u == 0 and b == 0:
                            act.wait_ge(pe_ada, 4)
                        wait(act, pe_pv, u)
                        nc.scalar.activation(pt[:, b, :], ring[:, 2:4, :], ACT.Exp,
                                             scale=DK ** -0.5).then_inc(act_exp, 1)

                    if u is not None:
                        exponentials(0)
                    if t == 2 and pair(g - 1):
                        wait(act, pe_ctxT, g)
                        nc.scalar.copy(ctxT[:, :], tbank[:, :]).then_inc(act_ctxT, 1)
                    if t == 3 and pair(g):
                        sums(g, 0)
                    if n is not None:
                        wait(act, l_st[t // 2], 16 * (g + 1))
                        nc.scalar.copy(w_hi[:, bass.ds(n * 512, 512)],
                                       stage[:, t // 2, t % 2 * 512:t % 2 * 512 + 512]).then_inc(act_hi, 1)
                    if t == 3 and pair(g + 1):
                        wait(act, pe_v, g + 2)
                        if isinstance(g, int) and g == -1:
                            act.wait_ge(pool_set, 1)
                        nc.scalar.copy(V[:, :, :, 0:DK],
                                       tbank[:, :].rearrange("p (k h d) -> p k h d", k=4, h=NH)).then_inc(act_v, 1)
                    if t == 3 and pair(g):
                        sums(g, 1)
                    if u is not None:
                        exponentials(1)
                    if isinstance(g, int) and g == NGR - 1 and t == 0:
                        act.wait_ge(pool_st, UNITS)
                        act.wait_ge(dve_x, 2)
                        row_sums(nc, norm1, X, 0, normal)
                    if isinstance(g, int) and g == NGR - 1 and t == 1:
                        row_squares(nc, act, norm1, X, 0, normal)

                run(act, step)

            @block.vector
            def _(dve):
                count = [0]

                def chain(ins):
                    count[0] += 1
                    ins.then_inc(set_done, 1)
                    dve.wait_ge(set_done, count[0])

                dve.wait_ge(pe_wT, 1)
                chain(dve.tensor_copy(wqoT[:, :, :], tbank[:, 0:256].rearrange("p (i n) -> p i n", i=2)))
                dve.tensor_copy(cndT[:, :, :], tbank[:, 256:256 + KT * B].rearrange("p (k n) -> p k n", k=KT)
                                ).then_inc(wT_done, 1)
                dve.wait_ge(pool_set, 1)
                wv = wst[:, :, :].rearrange("p j (s e d) -> p (j s) e d", s=2, d=DK)
                for slot in range(3):
                    last = dve.tensor_copy(wv[:, :, slot, :], wqoT[:, 0, :].rearrange("p (h d) -> p h d", h=NH))
                last.then_inc(wst_done, 1)
                def modulated():
                    dve.wait_ge(pe_ada, 4)
                    dve.wait_ge(l_small, 80)
                    chain(dve.tensor_tensor(ada[:, :, :], O[1][:, 0:12 * B].rearrange("p (m b) -> p m b", m=12),
                                            adab[:, :, None].to_broadcast([P, 12, B]), ALU.add))
                    chain(dve.tensor_scalar(ada[:, 2:4, :], ada[:, 2:4, :], 1.0, None, ALU.add))
                    chain(dve.tensor_scalar(ada[:, 8:10, :], ada[:, 8:10, :], 1.0, None, ALU.add))
                    chain(dve.tensor_tensor(gb1[:, :, :], ada[:, 4:6, :], ob[:, :, None].to_broadcast([P, KT, B]),
                                            ALU.mult))
                    chain(dve.tensor_tensor(gb2[:, :, :], ada[:, 10:12, :], b2[:, :, None].to_broadcast([P, KT, B]),
                                            ALU.mult))
                    dve.tensor_scalar(qb_s[:, :], qkvb[:, 0, :], SC, None, ALU.mult).then_inc(ada_done, 1)

                def step(g, t):
                    u, ju = unit(g, t, 1)
                    if u is not None:
                        wait(dve, pe_t, u + 1)
                        dve.tensor_tensor(qst2[:, :], tbank[:, :], qst[:, ju, :].bitcast(F32),
                                          ALU.add).then_inc(dve_q2, 1)
                    u2, _ = unit(g, t, 2)

                    def maxima(b):
                        wait(dve, pe_s, 2 * u2 + b + 1)
                        dst = mcol[:, 2 * b:2 * b + 2, :].rearrange("p q (s r) -> p s q r", s=2)[
                            :, :, :, ROWS_ONE + 1]
                        src = ring[:, 0:2, :].rearrange("p s (q k) -> p s q k", q=2)
                        dve.tensor_reduce(dst, src, AX_X, ALU.max, negate=True).then_inc(dve_max, 1)

                    if u2 is not None:
                        maxima(0)
                    u, ju = unit(g, t, 4)
                    if u is not None:
                        wait(dve, act_h, u + 1)
                        h = hs[:, :].bitcast(F32)
                        dve.scalar_tensor_tensor(qst[:, ju, :], h, cst[:, C_AQ:C_AQ + 1], vbank[:, :],
                                                 ALU.mult, ALU.add)
                        dve.scalar_tensor_tensor(kst[:, ju, :], h, cst[:, C_AK:C_AK + 1], vbank[:, :],
                                                 ALU.mult, ALU.add).then_inc(dve_st, 1)
                    if t < 2 and pair(g - 1):
                        wait(dve, pe_oT, 2 * g + t - 1)
                        ov = tbank[:, :].rearrange("p (h d) -> p h d", d=HP)
                        dve.reciprocal(rin[:, t, :], ov[:, :, DK]).then_inc(dve_rin, 1)
                        wait(dve, dve_rin, 2 * g + t - 1)
                        ctx_v = ctxs[:, 2 * t:2 * t + 2, :].rearrange("p q (f a n) -> p (q f) a n", f=2, a=2)
                        ov_v = ov.rearrange("p (x a e) d -> p x a e d", a=2, e=2)
                        rin_v = rin[:, t, :].rearrange("p (x a e) -> p x a e", a=2, e=2)
                        for a in range(2):
                            last = dve.tensor_tensor(ctx_v[:, :, (a + t) % 2, :].rearrange("p x (e d) -> p x e d", e=2),
                                                     ov_v[:, :, a, :, 0:DK],
                                                     rin_v[:, :, a, :, None].to_broadcast([P, 4, 2, DK]), ALU.mult)
                        last.then_inc(dve_ctx, 1)
                    if t == 3 and pair(g - 1):
                        wait(dve, pe_out, g)
                        xg = X[:, bass.ds(g * 2 - 2, 2), :]
                        dve.tensor_tensor(xg, tbank[:, :].rearrange("p (b d) -> p b d", b=2), xg,
                                          ALU.add).then_inc(dve_x, 1)
                    if u2 is not None:
                        maxima(1)
                    if isinstance(g, int) and g == -1 and t == 3:
                        modulated()
                    if isinstance(g, int) and g == NGR - 1 and t == 1:
                        row_means(dve, norm1, 0)
                    if isinstance(g, int) and g == NGR - 1 and t == 2:
                        deviations(dve, norm1, 0)
                        normal_rows(dve, norm1, normal, X, 0).then_inc(dve_n1, 1)

                run(dve, step)



def products(nc, bank, w_hi, w_lo, x_hi, x_lo, start, stop, ks):
    terms = [(w, x, k) for k in ks for w, x in ((w_hi, x_hi), (w_hi, x_lo), (w_lo, x_hi))]
    for i, (w, x, k) in enumerate(terms):
        last = nc.tensor.matmul(bank, w(k), x(k), start=(start and i == 0), stop=(stop and i == len(terms) - 1))
    return last


def split_input(w_hi, w_lo):
    return [w[:, X2_COL:X2_COL + KT * B * T].rearrange("p (k t) -> p k t", k=KT) for w in (w_hi, w_lo)]


def hidden(nc, bank, w_hi, w_lo, gn, cn):
    x2 = split_input(w_hi, w_lo)
    return products(nc, bank[:, :],
                    lambda k: w_hi[:, FFN_BLOCKS[k] + cn * P:FFN_BLOCKS[k] + (cn + 1) * P],
                    lambda k: w_lo[:, FFN_BLOCKS[k] + cn * P:FFN_BLOCKS[k] + (cn + 1) * P],
                    lambda k: x2[0][:, k, bass.ds(gn * GT, GT)],
                    lambda k: x2[1][:, k, bass.ds(gn * GT, GT)], True, True, range(KT))


def attention(nc, sem, sb, kept, saved, norm1, dve_n1, pe_n1, norm2, X, w_hi, w_lo, ada, gb1, qkvb, qb_s, ident,
              banks, ffn_w1, ffn_w2, x2f, act_x2, dve_x2, pe_f1):
    UN = NG * H
    Qb, Kb, Vb, Sb, Tb, Ob = banks[0:6]
    Yb = banks[6:8]
    with ExitStack() as ctx:
        x1f = sb(ctx, "x1f", [P, KT, GT])
        x1h = sb(ctx, "x1h", [P, KT, GT], F32R)
        x1l = sb(ctx, "x1l", [P, KT, GT], F32R)
        Q = sb(ctx, "Q", [P, 2, GT])
        K = sb(ctx, "K", [P, 2, GT])
        V = sb(ctx, "Vv", [P, 2, GB, 2 * DH])
        probs = sb(ctx, "probs", [P, 2, GB, T])
        pT = sb(ctx, "pT", [P, GT])
        oh = sb(ctx, "oh", [P, GT], F32R)
        ol = sb(ctx, "ol", [P, GT], F32R)
        yg = sb(ctx, "yg", [P, KT, GT])
        raw = sb(ctx, "raw", [P, 512])

        def xn(b):
            return yg[:, b // 2, b % 2 * DIM:(b % 2 + 1) * DIM]

        nm = sb(ctx, "nm", [P, 2, GB])
        sums = sb(ctx, "sums", [P, 2, GB])
        rinv = sb(ctx, "rinv", [P, 2, GB])
        (act_x1, dve_x1, pe_q, act_q, pe_k, act_k, pe_vv, dve_v, pe_sc, dve_mx, act_ex, dve_ri, pool_p, pe_pt, dve_pt,
         pe_o, act_oh, dve_ol, pe_y, act_y, dve_y, pe_yt, dve_xa, act_m1, dve_m1, dve_n2, pe_n2,
         act_m2, dve_m2, l_ffn, act_fhi, pool_flo) = (sem(n) for n in (
             "act_x1", "dve_x1", "pe_q", "act_q", "pe_k", "act_k", "pe_vv", "dve_v", "pe_sc", "dve_mx", "act_ex",
             "dve_ri", "pool_p", "pe_pt", "dve_pt", "pe_o", "act_oh", "dve_ol", "pe_y", "act_y", "dve_y", "pe_yt",
             "dve_xa", "act_m1", "dve_m1", "dve_n2", "pe_n2", "act_m2", "dve_m2", "l_ffn", "act_fhi",
             "pool_flo"))
        N1, N2 = (8, 9), (13, 14)

        def run(eng, step):
            step(-1, H - 1)
            for h in range(H):
                step(0, h)
            with eng.Fori(1, NG - 1) as g:
                for h in range(H):
                    step(g, h)
            for h in range(H):
                step(NG - 1, h)
            for h in range(4):
                step(NG, h)

        def unit(g, h, ahead):
            u = g * H + h + ahead
            if isinstance(u, int) and not 0 <= u < UN:
                return None
            return u

        def group(g):
            return not isinstance(g, int) or 0 <= g < NG

        with nc.Block() as block:

            @block.sync
            def _(sp):
                sp.dma_start(kept.rearrange("b p d -> p b d"), X[:, :, :]).then_inc(saved, 16)
                w2 = ffn_w2.rearrange("(c p) n -> p c n", p=P)
                for i in range(8):
                    if i:
                        sp.wait_ge(pool_flo, i)
                    k, half = divmod(i, 2)
                    if k < KT:
                        sp.dma_start(raw[:, :], ffn_w1[k * P:(k + 1) * P, half * 512:half * 512 + 512]
                                     ).then_inc(l_ffn, 16)
                    else:
                        c = (i - 2 * KT) * 2
                        sp.dma_start(raw[:, :].rearrange("p (c n) -> p c n", n=DIM), w2[:, c:c + 2, :]
                                     ).then_inc(l_ffn, 16)

            @block.tensor
            def _(pe):
                pe.wait_ge(act_m1, 1)
                pe.wait_ge(dve_m1, 1)

                def project(bank, part, hd):
                    def w(t):
                        return lambda k: t[:, k * 3 * INNER + part * INNER + hd * DH:
                                           k * 3 * INNER + part * INNER + (hd + 1) * DH]
                    return products(nc, bank[:, :], w(w_hi), w(w_lo), lambda k: x1h[:, k, :], lambda k: x1l[:, k, :],
                                    True, True, range(KT))

                def step(g, h):
                    n, prev, nxt = unit(g, h, 0), unit(g, h, -1), unit(g, h, 1)
                    hn = (h + 1) % H
                    if prev is not None:
                        wait(pe, pool_p, prev + 1)
                        wait(pe, dve_pt, prev)
                        if h in (3, 4) and group(g - 1):
                            wait(pe, dve_xa, 2 * g + h - 4)
                        if h - 1 in N1 and group(g + 1):
                            wait(pe, (act_m1, dve_m1)[h - 1 - N1[0]], g + 2)
                        if h - 1 in N2 and group(g - 1):
                            wait(pe, (act_m2, dve_m2)[h - 1 - N2[0]], g)
                        for b in range(GB):
                            last = nc.tensor.transpose(Tb[:, b * T:(b + 1) * T], probs[:, (h + 1) % 2, b, :], ident)
                        last.then_inc(pe_pt, 1)
                    if isinstance(g, int) and g == NG and h == 0:
                        hidden(nc, Kb, w_hi, w_lo, 0, 1).then_inc(pe_f1, 1)
                    if n is not None:
                        wait(pe, act_q, n + 1)
                        wait(pe, act_k, n + 1)
                        wait(pe, act_ex, n)
                        for b in range(GB):
                            t = slice(b * T, (b + 1) * T)
                            last = nc.tensor.matmul(Sb[:, t], Q[:, h % 2, t], K[:, h % 2, t], start=True, stop=True)
                        last.then_inc(pe_sc, 1)
                    if nxt is not None:
                        if hn == 0:
                            wait(pe, dve_x1, g + 2)
                        project(Qb, 0, hn).then_inc(pe_q, 1)
                    if prev is not None:
                        wait(pe, dve_pt, prev + 1)
                        wait(pe, dve_v, prev + (2 if h % 2 else 1))
                        wait(pe, dve_ol, prev)
                        for b in range(GB):
                            last = nc.tensor.matmul(Ob[:, b * T:(b + 1) * T],
                                                    V[:, (h - 1) % H // 2 % 2, b, (h + 1) % 2 * DH:
                                                      ((h + 1) % 2 + 1) * DH],
                                                    pT[:, b * T:(b + 1) * T], start=True, stop=True)
                        last.then_inc(pe_o, 1)
                    if isinstance(g, int) and g == NG - 1 and h == H - 1:
                        pe.wait_ge(dve_x2, 1)
                        pe.wait_ge(pool_flo, 4)
                        pe.wait_ge(act_k, UN)
                        hidden(nc, Qb, w_hi, w_lo, 0, 0).then_inc(pe_f1, 1)
                    if h in (2, 3) and group(g - 1):
                        wait(pe, act_y, g)
                        wait(pe, dve_y, g)
                        if h == 3:
                            wait(pe, dve_xa, 2 * g - 1)
                        for b in range(2):
                            for d in range(KT):
                                t0 = (2 * (h - 2) + b) * T
                                last = nc.tensor.transpose(Tb[:, b * DIM + d * P:b * DIM + (d + 1) * P],
                                                           yg[:, d, t0:t0 + T], ident)
                        last.then_inc(pe_yt, 1)
                    if h in N1 and group(g) and group(g + 1):
                        wait(pe, dve_n1, g + 2)
                        transposed(nc, ident, xn, h - N1[0], Tb).then_inc(pe_n1, 1)
                    if h in N2 and group(g) and group(g - 1):
                        wait(pe, dve_n2, g)
                        transposed(nc, ident, xn, h - N2[0], Tb).then_inc(pe_n2, 1)
                    if nxt is not None:
                        project(Kb, 1, hn).then_inc(pe_k, 1)
                        wait(pe, dve_v, nxt)
                        for i in range(2):
                            b = 2 * (hn % 2) + i
                            c0 = 2 * INNER + hn // 2 * 2 * DH
                            last = products(nc, Vb[:, i * 2 * DH:(i + 1) * 2 * DH],
                                            lambda k: x1h[:, k, b * T:(b + 1) * T],
                                            lambda k: x1l[:, k, b * T:(b + 1) * T],
                                            lambda k: w_hi[:, k * 3 * INNER + c0:k * 3 * INNER + c0 + 2 * DH],
                                            lambda k: w_lo[:, k * 3 * INNER + c0:k * 3 * INNER + c0 + 2 * DH],
                                            True, True, range(KT))
                        last.then_inc(pe_vv, 1)
                    if prev is not None:
                        hp = (h - 1) % H
                        wait(pe, dve_ol, prev + 1)
                        if hp == 0:
                            wait(pe, act_y, g)
                            wait(pe, dve_y, g)
                        for d in range(KT):
                            c = QKV_COLS + hp * DIM + d * P
                            last = products(nc, Yb[d][:, :], lambda k: w_hi[:, c:c + P], lambda k: w_lo[:, c:c + P],
                                            lambda k: oh[:, :], lambda k: ol[:, :], hp == 0, hp == H - 1, range(1))
                        last.then_inc(pe_y, 1)

                run(pe, step)

            @block.scalar
            def _(act):
                def modulate(dst, b0, scale, shift, done, bank=Tb):
                    for k in range(KT):
                        for b in range(2):
                            last = nc.scalar.activation(dst(k, b), bank[:, (2 * k + b) * P:(2 * k + b + 1) * P],
                                                        ACT.Identity, bias=ada[:, shift + k, bass.ds(b0 + b, 1)],
                                                        scale=ada[:, scale + k, bass.ds(b0 + b, 1)])
                    last.then_inc(done, 1)

                act.wait_ge(pe_n1, 1)
                modulate(lambda k, b: x1f[:, k, b * T:(b + 1) * T], 0, 2, 0, act_m1, Qb)

                def step(g, h):
                    n, prev, nxt = unit(g, h, 0), unit(g, h, -1), unit(g, h, 1)
                    hn = (h + 1) % H
                    if h == H - 1 and group(g + 1):
                        wait(act, pe_vv, H * (g + 1))
                        wait(act, act_m1, g + 2)
                        wait(act, dve_m1, g + 2)
                        nc.scalar.copy(x1h[:, :, :], x1f[:, :, :]).then_inc(act_x1, 1)
                    if h == 1 and group(g - 1):
                        wait(act, pe_y, H * g)
                        for b in range(GB):
                            last = nc.scalar.activation(yg[:, 0, b * T:(b + 1) * T], Yb[0][:, b * T:(b + 1) * T],
                                                        ACT.Identity, bias=gb1[:, 0, bass.ds((g - 1) * GB + b, 1)],
                                                        scale=ada[:, 4, bass.ds((g - 1) * GB + b, 1)])
                        last.then_inc(act_y, 1)
                    if isinstance(g, int) and g == NG - 1 and h == H - 1:
                        act.wait_ge(pe_vv, UN)
                        act.wait_ge(dve_m2, NG - 1)
                        nc.scalar.copy(split_input(w_hi, w_lo)[0][:, :, 0:GT], x2f[:, :, 0:GT]).then_inc(act_x2, 1)
                    if isinstance(g, int) and g == NG and h == 1:
                        nc.scalar.activation(norm2.taken[:, :], norm2.mean[:, 0:1], ACT.Gelu)
                    if n is not None:
                        wait(act, dve_mx, n + 1)
                        wait(act, pe_pt, n - 1)
                        for b in range(GB):
                            last = nc.scalar.activation(probs[:, h % 2, b, :], Sb[:, b * T:(b + 1) * T], ACT.Exp,
                                                        bias=nm[:, h % 2, b:b + 1],
                                                        accum_out=sums[:, h % 2, b:b + 1])
                        last.then_inc(act_ex, 1)
                    if prev is not None:
                        wait(act, pe_o, prev + 1)
                        nc.scalar.activation(oh[:, :], Ob[:, :], ACT.Identity,
                                             bias=qkvb[:, 2, (h - 1) % H:(h - 1) % H + 1]).then_inc(act_oh, 1)
                    if h == N1[0] and group(g) and group(g + 1):
                        wait(act, pe_n1, 2 * g + 3)
                        wait(act, dve_x1, g + 1)
                        modulate(lambda k, b: x1f[:, k, b * T:(b + 1) * T], (g + 1) * GB, 2, 0, act_m1)
                    if h == N2[0] and group(g) and group(g - 1):
                        wait(act, pe_n2, 2 * g - 1)
                        modulate(lambda k, b: x2f[:, k, bass.ds((g - 1) * GT + b * T, T)],
                                 (g - 1) * GB, 8, 6, act_m2)
                    if nxt is not None:
                        wait(act, pe_q, nxt + 1)
                        nc.scalar.activation(Q[:, hn % 2, :], Qb[:, :], ACT.Identity, bias=qb_s[:, hn:hn + 1],
                                             scale=SC).then_inc(act_q, 1)
                        wait(act, pe_k, nxt + 1)
                        nc.scalar.activation(K[:, hn % 2, :], Kb[:, :], ACT.Identity,
                                             bias=qkvb[:, 1, hn:hn + 1]).then_inc(act_k, 1)
                    if group(g) and group(g + 1):
                        if h == N1[0] - 4:
                            if group(g - 1):
                                wait(act, pe_yt, 2 * g)
                            row_sums(nc, norm1, X, g + 1, xn)
                        if h == N1[0] - 3:
                            row_squares(nc, act, norm1, X, g + 1, xn)
                    if group(g) and group(g - 1):
                        if h == N2[0] - 4:
                            wait(act, dve_xa, 2 * g)
                            if group(g + 1):
                                wait(act, pe_n1, 2 * g + 4)
                            row_sums(nc, norm2, X, g - 1, xn)
                        if h == N2[0] - 3:
                            row_squares(nc, act, norm2, X, g - 1, xn)
                    if isinstance(g, int) and g == NG - 1 and h >= H - 8:
                        i = h - (H - 8)
                        if i == 0:
                            act.wait_ge(pe_vv, UN - 8)
                        act.wait_ge(l_ffn, 16 * (i + 1))
                        c0 = FFN_BLOCKS[i // 2] + i % 2 * 512
                        nc.scalar.copy(w_hi[:, c0:c0 + 512], raw[:, :]).then_inc(act_fhi, 1)

                run(act, step)

            @block.vector
            def _(dve):
                def modulate(dst, b0, scale, shift, done):
                    for k in range(KT):
                        for b in range(2):
                            last = dve.tensor_scalar(dst(k, b), Tb[:, (2 * k + b) * P:(2 * k + b + 1) * P],
                                                     ada[:, scale + k, bass.ds(b0 + b, 1)],
                                                     ada[:, shift + k, bass.ds(b0 + b, 1)], ALU.mult, ALU.add)
                    last.then_inc(done, 1)

                dve.wait_ge(pe_n1, 2)
                modulate(lambda k, b: x1f[:, k, (2 + b) * T:(3 + b) * T], 2, 2, 0, dve_m1)

                def step(g, h):
                    n, prev, nxt = unit(g, h, 0), unit(g, h, -1), unit(g, h, 1)
                    hn = (h + 1) % H
                    if h == H - 1 and group(g + 1):
                        wait(dve, act_x1, g + 2)
                        dve.tensor_tensor(x1l[:, :, :], x1f[:, :, :],
                                          x1h[:, :, :].bitcast(F32), ALU.subtract).then_inc(dve_x1, 1)
                    if prev is not None:
                        wait(dve, pe_pt, prev + 1)
                        dve.tensor_copy(pT[:, :], Tb[:, :]).then_inc(dve_pt, 1)
                    if h == 1 and group(g - 1):
                        wait(dve, pe_y, H * g)
                        for b in range(GB):
                            last = dve.tensor_scalar(yg[:, 1, b * T:(b + 1) * T], Yb[1][:, b * T:(b + 1) * T],
                                                     ada[:, 5, bass.ds((g - 1) * GB + b, 1)],
                                                     gb1[:, 1, bass.ds((g - 1) * GB + b, 1)], ALU.mult, ALU.add)
                        last.then_inc(dve_y, 1)
                    if n is not None:
                        wait(dve, pe_sc, n + 1)
                        dve.tensor_reduce(nm[:, h % 2, :], Sb[:, :].rearrange("p (b k) -> p b k", b=GB), AX_X,
                                          ALU.max, negate=True).then_inc(dve_mx, 1)
                        if isinstance(g, int) and g == NG - 1 and h == H - 1:
                            dve.wait_ge(act_x2, 1)
                            x2 = split_input(w_hi, w_lo)
                            dve.tensor_tensor(x2[1][:, :, 0:GT], x2f[:, :, 0:GT], x2[0][:, :, 0:GT].bitcast(F32),
                                              ALU.subtract).then_inc(dve_x2, 1)
                        wait(dve, act_ex, n + 1)
                        dve.reciprocal(rinv[:, h % 2, :], sums[:, h % 2, :]).then_inc(dve_ri, 1)
                    if prev is not None:
                        wait(dve, act_oh, prev + 1)
                        dve.scalar_tensor_tensor(ol[:, :], Ob[:, :], qkvb[:, 2, (h - 1) % H:(h - 1) % H + 1],
                                                 oh[:, :].bitcast(F32), ALU.add, ALU.subtract).then_inc(dve_ol, 1)
                    if h == N1[1] and group(g) and group(g + 1):
                        wait(dve, pe_n1, 2 * g + 4)
                        modulate(lambda k, b: x1f[:, k, (2 + b) * T:(3 + b) * T], (g + 1) * GB + 2, 2, 0, dve_m1)
                    if h == N2[1] and group(g) and group(g - 1):
                        wait(dve, pe_n2, 2 * g)
                        modulate(lambda k, b: x2f[:, k, bass.ds((g - 1) * GT + (2 + b) * T, T)],
                                 (g - 1) * GB + 2, 8, 6, dve_m2)
                    if h in (2, 3) and group(g - 1):
                        wait(dve, pe_yt, 2 * g + h - 3)
                        if h == 2:
                            dve.wait_ge(saved, 16)
                        xg = X[:, bass.ds((g - 1) * GB + 2 * (h - 2), 2), :]
                        dve.tensor_tensor(xg, Tb[:, :].rearrange("p (b d) -> p b d", b=2), xg,
                                          ALU.add).then_inc(dve_xa, 1)
                    if nxt is not None:
                        wait(dve, pe_vv, nxt + 1)
                        dve.tensor_copy(V[:, hn // 2 % 2, 2 * (hn % 2):2 * (hn % 2) + 2, :],
                                        Vb[:, :].rearrange("p (b d) -> p b d", b=2)).then_inc(dve_v, 1)
                    if group(g) and group(g + 1):
                        if h == N1[0] - 4:
                            row_means(dve, norm1, g + 1)
                        if h == N1[0] - 2:
                            deviations(dve, norm1, g + 1)
                        if h == N1[0] - 1:
                            normal_rows(dve, norm1, xn, X, g + 1).then_inc(dve_n1, 1)
                    if group(g) and group(g - 1):
                        if h == N2[0] - 4:
                            row_means(dve, norm2, g - 1)
                        if h == N2[0] - 2:
                            deviations(dve, norm2, g - 1)
                        if h == N2[0] - 1:
                            normal_rows(dve, norm2, xn, X, g - 1).then_inc(dve_n2, 1)
                run(dve, step)

            @block.gpsimd
            def _(pool):
                def step(g, h):
                    n = unit(g, h, 0)
                    if n is not None:
                        wait(pool, dve_ri, n + 1)
                        pool.tensor_tensor(probs[:, h % 2, :, :], probs[:, h % 2, :, :],
                                           rinv[:, h % 2, :, None].to_broadcast([P, GB, T]),
                                           ALU.mult).then_inc(pool_p, 1)
                    if isinstance(g, int) and g == NG - 1 and h >= H - 8:
                        i = h - (H - 8)
                        c0 = FFN_BLOCKS[i // 2] + i % 2 * 512
                        pool.wait_ge(act_fhi, i + 1)
                        pool.tensor_tensor(w_lo[:, c0:c0 + 512], raw[:, :], w_hi[:, c0:c0 + 512].bitcast(F32),
                                           ALU.subtract).then_inc(pool_flo, 1)

                run(pool, step)


def ffn(nc, sem, sb, kept, norm2, x2f, act_x2, dve_x2, pe_f1, X, w_hi, w_lo, ada, gb2, b1, ident, banks, out):
    UN = NG * MC
    Hb, Yb, Tb, Nb = banks[0:2], banks[2:4], banks[4:6], banks[6:8]
    x2 = split_input(w_hi, w_lo)
    hid = [w[:, HID_COL:HID_COL + 4 * GT].rearrange("p (s t) -> p s t", s=4) for w in (w_hi, w_lo)]
    with ExitStack() as ctx:
        hf = sb(ctx, "hf", [P, 2, GT])
        yg = sb(ctx, "yg2", [P, KT, GT])
        xk = sb(ctx, "xk", [P, B, DIM])
        xn_t = sb(ctx, "xn", [P, GB, DIM])

        def xn(b):
            return xn_t[:, b, :]

        l_xk = sem("l_xk")
        dve_n, pe_n, act_m, dve_m = (sem(n) for n in ("dve_n", "pe_n", "act_m", "dve_m"))
        act_g, act_hh, dve_hl, pe_f2, act_y2, dve_y2, pe_y2t, dve_xo, stored = (
            sem(n) for n in ("act_g", "act_hh", "dve_hl", "pe_f2", "act_y2", "dve_y2",
                             "pe_y2t", "dve_xo", "stored"))

        def run(eng, step):
            for c in range(MC - 2, MC):
                step(-1, c)
            for c in range(MC):
                step(0, c)
            with eng.Fori(1, NG - 1) as g:
                for c in range(MC):
                    step(g, c)
            for c in range(MC):
                step(NG - 1, c)
            for c in range(2):
                step(NG, c)

        def unit(g, c, ahead):
            u = g * MC + c + ahead
            if isinstance(u, int) and not 0 <= u < UN:
                return None
            return u

        def group(g):
            return not isinstance(g, int) or 0 <= g < NG

        with nc.Block() as block:

            @block.tensor
            def _(pe):
                def step(g, c):
                    m, nxt = unit(g, c, 0), unit(g, c, 2)
                    cn = (c + 2) % MC
                    gn = g + (c + 2) // MC
                    if nxt is not None and not (isinstance(g, int) and g == -1):
                        if cn == 0:
                            wait(pe, dve_x2, gn + 1)
                        wait(pe, act_g, nxt - 1)
                        hidden(nc, Hb[c % 2], w_hi, w_lo, gn, cn).then_inc(pe_f1, 1)
                    if m is not None:
                        wait(pe, dve_hl, m + 1)
                        if c == 0:
                            wait(pe, act_y2, g)
                            wait(pe, dve_y2, g)
                        for d in range(KT):
                            c0 = FFN_BLOCKS[KT + c // 4] + c % 4 * DIM + d * P
                            last = products(nc, Yb[d][:, :], lambda k: w_hi[:, c0:c0 + P],
                                            lambda k: w_lo[:, c0:c0 + P], lambda k: hid[0][:, c % 4, :],
                                            lambda k: hid[1][:, c % 4, :], c == 0, c == MC - 1, range(1))
                        last.then_inc(pe_f2, 1)
                    if c == 1 and group(g - 1):
                        wait(pe, act_y2, g)
                        wait(pe, dve_y2, g)
                        for b in range(GB):
                            for d in range(KT):
                                last = nc.tensor.transpose(
                                    Tb[b // 2][:, b % 2 * DIM + d * P:b % 2 * DIM + (d + 1) * P],
                                    yg[:, d, b * T:(b + 1) * T], ident)
                        last.then_inc(pe_y2t, 1)
                    if isinstance(g, int) and g == 0 and c == 7:
                        pe.wait_ge(dve_n, 1)
                        for b in range(GB):
                            for k in range(KT):
                                last = nc.tensor.transpose(Nb[k][:, b * T:(b + 1) * T], xn(b)[:, k * P:(k + 1) * P],
                                                           ident)
                        last.then_inc(pe_n, 1)

                run(pe, step)

            @block.scalar
            def _(act):
                def split(g):
                    nc.scalar.copy(x2[0][:, :, bass.ds(g * GT, GT)], x2f[:, :, bass.ds(g * GT, GT)]
                                   ).then_inc(act_x2, 1)

                def step(g, c):
                    if c == 0 and group(g - 1):
                        wait(act, pe_f2, MC * g)
                        for b in range(GB):
                            last = nc.scalar.activation(yg[:, 0, b * T:(b + 1) * T], Yb[0][:, b * T:(b + 1) * T],
                                                        ACT.Identity, bias=gb2[:, 0, bass.ds((g - 1) * GB + b, 1)],
                                                        scale=ada[:, 10, bass.ds((g - 1) * GB + b, 1)])
                        last.then_inc(act_y2, 1)
                    nxt = unit(g, c, 2)
                    if nxt is not None:
                        cn = (c + 2) % MC
                        wait(act, pe_f1, nxt + 1)
                        wait(act, dve_hl, nxt - 1)
                        nc.scalar.activation(hf[:, c % 2, :], Hb[c % 2][:, :], ACT.Gelu,
                                             bias=b1[:, cn:cn + 1]).then_inc(act_g, 1)
                        wait(act, act_g, nxt + 1)
                        nc.scalar.copy(hid[0][:, cn % 4, :], hf[:, c % 2, :]).then_inc(act_hh, 1)
                    if isinstance(g, int) and g == 0 and c == 1:
                        row_sums(nc, norm2, X, NG - 1, xn)
                    if isinstance(g, int) and g == 0 and c == 2:
                        row_squares(nc, act, norm2, X, NG - 1, xn)
                    if isinstance(g, int) and g == 0 and c == 7:
                        act.wait_ge(pe_n, 1)
                        for b in range(GB):
                            t0 = (NG - 1) * GT + b * T
                            last = nc.scalar.activation(x2f[:, 0, t0:t0 + T], Nb[0][:, b * T:(b + 1) * T],
                                                        ACT.Identity, bias=ada[:, 6, B - GB + b:B - GB + b + 1],
                                                        scale=ada[:, 8, B - GB + b:B - GB + b + 1])
                        last.then_inc(act_m, 1)
                    if c == 3 and group(g + 1) and group(g):
                        if isinstance(g, int) and g + 1 == NG - 1:
                            act.wait_ge(dve_m, 1)
                        split(g + 1)

                run(act, step)

            @block.vector
            def _(dve):
                def split(g):
                    wait(dve, act_x2, g + 1)
                    dve.tensor_tensor(x2[1][:, :, bass.ds(g * GT, GT)], x2f[:, :, bass.ds(g * GT, GT)],
                                      x2[0][:, :, bass.ds(g * GT, GT)].bitcast(F32),
                                      ALU.subtract).then_inc(dve_x2, 1)

                def step(g, c):
                    if c == 0 and group(g - 1):
                        wait(dve, pe_f2, MC * g)
                        for b in range(GB):
                            last = dve.tensor_scalar(yg[:, 1, b * T:(b + 1) * T], Yb[1][:, b * T:(b + 1) * T],
                                                     ada[:, 11, bass.ds((g - 1) * GB + b, 1)],
                                                     gb2[:, 1, bass.ds((g - 1) * GB + b, 1)], ALU.mult, ALU.add)
                        last.then_inc(dve_y2, 1)
                    nxt = unit(g, c, 2)
                    if nxt is not None:
                        cn = (c + 2) % MC
                        wait(dve, act_hh, nxt + 1)
                        dve.tensor_tensor(hid[1][:, cn % 4, :], hf[:, c % 2, :], hid[0][:, cn % 4, :].bitcast(F32),
                                          ALU.subtract).then_inc(dve_hl, 1)
                    if c == 1 and group(g - 1):
                        wait(dve, pe_y2t, g)
                        for i in range(2):
                            xg = X[:, bass.ds((g - 1) * GB + 2 * i, 2), :]
                            last = dve.tensor_tensor(xg, Tb[i][:, :].rearrange("p (b d) -> p b d", b=2), xg, ALU.add)
                        last.then_inc(dve_xo, 1)
                    if c == 3 and group(g + 1) and group(g):
                        split(g + 1)
                    if isinstance(g, int) and g == 0:
                        if c == 1:
                            row_means(dve, norm2, NG - 1)
                        if c == 5:
                            deviations(dve, norm2, NG - 1)
                        if c == 6:
                            normal_rows(dve, norm2, xn, X, NG - 1).then_inc(dve_n, 1)
                        if c == 7:
                            dve.wait_ge(pe_n, 1)
                            for b in range(GB):
                                t0 = (NG - 1) * GT + b * T
                                last = dve.tensor_scalar(x2f[:, 1, t0:t0 + T], Nb[1][:, b * T:(b + 1) * T],
                                                         ada[:, 9, B - GB + b:B - GB + b + 1],
                                                         ada[:, 7, B - GB + b:B - GB + b + 1], ALU.mult, ALU.add)
                            last.then_inc(dve_m, 1)
                    if c == 2 and group(g):
                        dve.wait_ge(l_xk, 16)
                        xg = X[:, bass.ds(g * GB, GB), :]
                        dve.tensor_tensor(xg, xk[:, bass.ds(g * GB, GB), :], xg, ALU.add)

                run(dve, step)

            @block.sync
            def _(sp):
                sp.dma_start(xk[:, :, :], kept.rearrange("b p d -> p b d")).then_inc(l_xk, 16)
                for g in range(NG):
                    sp.wait_ge(dve_xo, g + 1)
                    sp.dma_start(out[g * GB:(g + 1) * GB].rearrange("b p d -> p b d"),
                                 X[:, g * GB:(g + 1) * GB, :]).then_inc(stored, 16)
                sp.wait_ge(stored, 16 * NG)


_INS = ["x", "cond_2048", "L0_cond_Wq", "L0_cond_Wo", "L1_cond_ada_w", "L1_cond_ada_b", "L1_cond_qkv_w",
        "L1_cond_qkv_b", "L1_cond_out_w", "L1_cond_out_b", "L1_cond_ffn_w1", "L1_cond_ffn_b1", "L1_cond_ffn_w2",
        "L1_cond_ffn_b2"]


def constants(np):
    c = np.zeros((P, C_ID + P), np.float32)
    c[:, C_ID:] = np.eye(P, dtype=np.float32)
    c[:, C_RA] = c[:, C_CA] = 1.0
    for r in (0, 64):
        c[r + DK:r + 2 * DK, C_AQ] = -1.0
        c[r + 2 * DK:r + 3 * DK, C_AK] = -1.0
        one = r + ROWS_ONE
        c[one:one + 2, C_BH] = c[one:one + 2, C_AQ] = c[one:one + 2, C_AK] = 1.0
        c[one, C_CA], c[one, C_CB] = -NEG * DK ** 0.5, NEG * DK ** 0.5
        c[one + 1, C_RA], c[one + 1, C_CA], c[one + 1, C_CB] = 0.0, 0.0, 1.0
    return c


def kernel(**inputs):
    import numpy as _np
    import concourse.bacc as _bacc
    from concourse import mybir as _mybir
    from concourse.bass_utils import run_bass_kernel_spmd as _run

    nc = _bacc.Bacc("TRN2", target_bir_lowering=False, num_devices=1)
    arrays, args = {}, []
    for name in _INS:
        a = _np.ascontiguousarray(inputs[name])
        arrays[f"in_{name}_dram"] = a
        args.append(nc.dram_tensor(f"in_{name}_dram", a.shape, _mybir.dt.from_np(a.dtype), kind="ExternalInput").ap())
    arrays["stack_constants"] = constants(_np)
    args.append(nc.dram_tensor("stack_constants", (P, C_ID + P), F32, kind="ExternalInput").ap())
    out = nc.dram_tensor("out_dram", (B, T, DIM), F32, kind="ExternalOutput").ap()
    build(nc, *args, out)
    r = _run(nc, [arrays], core_ids=[0])
    return r.results[0]["out_dram"]
```
